# Optimizing a Trainium2 kernel written in Bass

```python
import numpy as np
import jax
import jax.numpy as jnp

def _softmax(x, axis=-1):
    return jax.nn.softmax(x, axis=axis)
def _gelu(x):
    return jax.nn.gelu(x, approximate=True)
def _silu(x):
    return jax.nn.silu(x)
def _sigmoid(x):
    return jax.nn.sigmoid(x)
def _layernorm(x, axis=-1, eps=1e-5):
    m = jnp.mean(x, axis=axis, keepdims=True)
    v = jnp.var(x, axis=axis, keepdims=True)
    return (x - m) / jnp.sqrt(v + eps)
def _scatter_add(tgt, idx, src, axis=0):
    return tgt.at[idx].add(src)
def _segment_sum(src, seg, n):
    return jax.ops.segment_sum(src, seg, n)

kernel_name = 'mk_metaformer_d1_conv_nchw384_0df0a3'

def setup_inputs(seed: int = 0):
    np.random.seed(seed)
    _w = jnp.asarray
    def _rec_inputs():
        import jax
        import jax.numpy as jnp
        _gk = jax.random.key(seed)
        x = -0.0005963 + 1.001 * jax.random.normal(jax.random.fold_in(_gk, 1), (8, 384, 32, 32), jnp.float32)
        return x
    x = _rec_inputs()
    def _L0_conv_setup():
        import jax, jax.numpy as jnp
        import numpy as np
        B, C, H, W = (8, 384, 32, 32)
        NUM_HEADS = 8
        HEAD_DIM = C // NUM_HEADS
        HIDDEN = max(32, C // 2)

        def _relative_bias(h, w, mlp_w1, mlp_b1, mlp_w2, mlp_b2):
            ch = jnp.arange(h, dtype=jnp.float32)
            cw = jnp.arange(w, dtype=jnp.float32)
            coords = jnp.stack(jnp.meshgrid(ch, cw, indexing='ij'), axis=-1).reshape(-1, 2)
            rel = coords[:, None, :] - coords[None, :, :]
            denom = jnp.array([max(h - 1, 1), max(w - 1, 1)], dtype=jnp.float32)
            rel = rel / denom
            hidden = jax.nn.gelu(rel @ mlp_w1 + mlp_b1, approximate=False)
            bias = hidden @ mlp_w2 + mlp_b2
            return jnp.transpose(bias, (2, 0, 1))
        key = jax.random.key(seed)
        ks = jax.random.split(key, 6)
        s = lambda fan_in: 1.0 / np.sqrt(fan_in)
        return {'x': jax.random.normal(ks[0], (B, C, H, W), dtype=jnp.float32), 'qkv_w': jax.random.normal(ks[1], (C, 3 * C), dtype=jnp.float32) * s(C), 'qkv_b': jnp.zeros((3 * C,), dtype=jnp.float32), 'proj_w': jax.random.normal(ks[2], (C, C), dtype=jnp.float32) * s(C), 'proj_b': jnp.zeros((C,), dtype=jnp.float32), 'mlp_w1': jax.random.normal(ks[3], (2, HIDDEN), dtype=jnp.float32) * s(2), 'mlp_b1': jnp.zeros((HIDDEN,), dtype=jnp.float32), 'mlp_w2': jax.random.normal(ks[4], (HIDDEN, NUM_HEADS), dtype=jnp.float32) * s(HIDDEN), 'mlp_b2': jnp.zeros((NUM_HEADS,), dtype=jnp.float32)}
    _L0_conv_all = _L0_conv_setup()
    _L0_conv_in = {k: v for k, v in _L0_conv_all.items() if k in ('qkv_w', 'qkv_b', 'proj_w', 'proj_b', 'mlp_w1', 'mlp_b1', 'mlp_w2', 'mlp_b2', )}
    del _L0_conv_all

    def _L0_ffn_setup():
        import jax, jax.numpy as jnp
        import numpy as np
        NUM_GROUPS = 5
        EPS = 1e-05
        QB = 128.0

        def _binarize_weights_groupwise(W):
            n_out = W.shape[0]
            gs = n_out // NUM_GROUPS
            Wb = jnp.zeros_like(W)
            for g in range(NUM_GROUPS):
                wg = W[g * gs:(g + 1) * gs]
                z = wg - wg.mean()
                ste = z + jax.lax.stop_gradient(jnp.sign(z) - z)
                Wb = Wb.at[g * gs:(g + 1) * gs].set(ste)
            return Wb

        def _quantize_activations_groupwise(x):
            n = x.shape[0]
            gs = n // NUM_GROUPS
            xq = jnp.zeros_like(x)
            for g in range(NUM_GROUPS):
                ag = x[g * gs:(g + 1) * gs]
                gamma = jnp.max(jnp.abs(ag))
                xq = xq.at[g * gs:(g + 1) * gs].set(jnp.clip(ag * QB / (gamma + EPS), -QB + EPS, QB - EPS))
            return xq

        def _bitlinear(x, W, b):
            Wb = _binarize_weights_groupwise(W)
            y = jnp.einsum('btc,oc->bto', x, Wb) + b
            return _quantize_activations_groupwise(y)
        key = jax.random.key(seed)
        k1, k2, k3, k4, k5 = jax.random.split(key, 5)
        B, T, C = (10, 2048, 384)
        H = 4 * C
        lim1 = 1.0 / np.sqrt(C)
        lim2 = 1.0 / np.sqrt(H)
        x = jax.random.normal(k1, (B, T, C), dtype=jnp.float32)
        W1 = jax.random.uniform(k2, (H, C), minval=-lim1, maxval=lim1, dtype=jnp.float32)
        b1 = jax.random.uniform(k3, (H,), minval=-lim1, maxval=lim1, dtype=jnp.float32)
        W2 = jax.random.uniform(k4, (C, H), minval=-lim2, maxval=lim2, dtype=jnp.float32)
        b2 = jax.random.uniform(k5, (C,), minval=-lim2, maxval=lim2, dtype=jnp.float32)
        return {'x': x, 'W1': W1, 'b1': b1, 'W2': W2, 'b2': b2}
    _L0_ffn_all = _L0_ffn_setup()
    _L0_ffn_in = {k: v for k, v in _L0_ffn_all.items() if k in ('W1', 'b1', 'W2', 'b2', )}
    del _L0_ffn_all

    return {
        "x": x,
        "L0_conv_qkv_w": _L0_conv_in["qkv_w"],
        "L0_conv_qkv_b": _L0_conv_in["qkv_b"],
        "L0_conv_proj_w": _L0_conv_in["proj_w"],
        "L0_conv_proj_b": _L0_conv_in["proj_b"],
        "L0_conv_mlp_w1": _L0_conv_in["mlp_w1"],
        "L0_conv_mlp_b1": _L0_conv_in["mlp_b1"],
        "L0_conv_mlp_w2": _L0_conv_in["mlp_w2"],
        "L0_conv_mlp_b2": _L0_conv_in["mlp_b2"],
        "L0_ffn_W1": _L0_ffn_in["W1"],
        "L0_ffn_b1": _L0_ffn_in["b1"],
        "L0_ffn_W2": _L0_ffn_in["W2"],
        "L0_ffn_b2": _L0_ffn_in["b2"],
    }

def reference(x, L0_conv_qkv_w, L0_conv_qkv_b, L0_conv_proj_w, L0_conv_proj_b, L0_conv_mlp_w1, L0_conv_mlp_b1, L0_conv_mlp_w2, L0_conv_mlp_b2, L0_ffn_W1, L0_ffn_b1, L0_ffn_W2, L0_ffn_b2):
    import jax
    import jax.numpy as jnp
    def _L0_conv_ref(x, qkv_w, qkv_b, proj_w, proj_b, mlp_w1, mlp_b1, mlp_w2, mlp_b2):
        import jax, jax.numpy as jnp
        import numpy as np
        B, C, H, W = (8, 384, 32, 32)
        NUM_HEADS = 8
        HEAD_DIM = C // NUM_HEADS
        HIDDEN = max(32, C // 2)

        def _relative_bias(h, w, mlp_w1, mlp_b1, mlp_w2, mlp_b2):
            ch = jnp.arange(h, dtype=jnp.float32)
            cw = jnp.arange(w, dtype=jnp.float32)
            coords = jnp.stack(jnp.meshgrid(ch, cw, indexing='ij'), axis=-1).reshape(-1, 2)
            rel = coords[:, None, :] - coords[None, :, :]
            denom = jnp.array([max(h - 1, 1), max(w - 1, 1)], dtype=jnp.float32)
            rel = rel / denom
            hidden = jax.nn.gelu(rel @ mlp_w1 + mlp_b1, approximate=False)
            bias = hidden @ mlp_w2 + mlp_b2
            return jnp.transpose(bias, (2, 0, 1))
        b, c, h, w = x.shape
        n = h * w
        tokens = x.reshape(b, c, n).transpose(0, 2, 1)
        qkv = (tokens @ qkv_w + qkv_b).reshape(b, n, 3, NUM_HEADS, HEAD_DIM)
        qkv = jnp.transpose(qkv, (2, 0, 3, 1, 4))
        q, k, v = (qkv[0], qkv[1], qkv[2])
        scale = HEAD_DIM ** (-0.5)
        attn = jnp.einsum('bhnd,bhmd->bhnm', q * scale, k)
        attn = attn + _relative_bias(h, w, mlp_w1, mlp_b1, mlp_w2, mlp_b2)[None]
        attn = jax.nn.softmax(attn, axis=-1)
        out = jnp.einsum('bhnm,bhmd->bhnd', attn, v)
        out = out.transpose(0, 2, 1, 3).reshape(b, n, c)
        out = out @ proj_w + proj_b
        return out.transpose(0, 2, 1).reshape(b, c, h, w)

    def _L0_ffn_ref(x, W1, b1, W2, b2):
        import jax, jax.numpy as jnp
        import numpy as np
        NUM_GROUPS = 5
        EPS = 1e-05
        QB = 128.0

        def _binarize_weights_groupwise(W):
            n_out = W.shape[0]
            gs = n_out // NUM_GROUPS
            Wb = jnp.zeros_like(W)
            for g in range(NUM_GROUPS):
                wg = W[g * gs:(g + 1) * gs]
                z = wg - wg.mean()
                ste = z + jax.lax.stop_gradient(jnp.sign(z) - z)
                Wb = Wb.at[g * gs:(g + 1) * gs].set(ste)
            return Wb

        def _quantize_activations_groupwise(x):
            n = x.shape[0]
            gs = n // NUM_GROUPS
            xq = jnp.zeros_like(x)
            for g in range(NUM_GROUPS):
                ag = x[g * gs:(g + 1) * gs]
                gamma = jnp.max(jnp.abs(ag))
                xq = xq.at[g * gs:(g + 1) * gs].set(jnp.clip(ag * QB / (gamma + EPS), -QB + EPS, QB - EPS))
            return xq

        def _bitlinear(x, W, b):
            Wb = _binarize_weights_groupwise(W)
            y = jnp.einsum('btc,oc->bto', x, Wb) + b
            return _quantize_activations_groupwise(y)
        h = _bitlinear(x, W1, b1)
        h = jax.nn.gelu(h, approximate=False)
        out = _bitlinear(h, W2, b2)
        return out

    def _gn(v, G=32, eps=1e-5):
        B_, C_, H_, W_ = v.shape
        g = v.reshape(B_, G, C_ // G, H_, W_)
        m = jnp.mean(g, axis=(2, 3, 4), keepdims=True)
        s = jnp.var(g, axis=(2, 3, 4), keepdims=True)
        return ((g - m) / jnp.sqrt(s + eps)).reshape(v.shape)

    def _ln_c(v, eps=1e-6):
        m = jnp.mean(v, axis=1, keepdims=True)
        s = jnp.var(v, axis=1, keepdims=True)
        return (v - m) / jnp.sqrt(s + eps)

    def _ln_t(v, eps=1e-5):
        m = jnp.mean(v, axis=-1, keepdims=True)
        s = jnp.var(v, axis=-1, keepdims=True)
        return (v - m) / jnp.sqrt(s + eps)

    def _to_tokens(v):
        B_, C_, H_, W_ = v.shape
        return v.reshape(B_, C_, H_ * W_).transpose(0, 2, 1)
    def _from_tokens(t, like):
        B_, C_, H_, W_ = like.shape
        return t.transpose(0, 2, 1).reshape(B_, C_, H_, W_)

    x = x + _L0_conv_ref(_ln_c(x), L0_conv_qkv_w, L0_conv_qkv_b, L0_conv_proj_w, L0_conv_proj_b, L0_conv_mlp_w1, L0_conv_mlp_b1, L0_conv_mlp_w2, L0_conv_mlp_b2)
    t = _to_tokens(x)
    t = t + _L0_ffn_ref(_ln_t(t), L0_ffn_W1, L0_ffn_b1, L0_ffn_W2, L0_ffn_b2)
    x = _from_tokens(t, x)
    return x


_drawn_inputs = setup_inputs


def setup_inputs(seed=0):
    import zlib

    import numpy as np

    out = dict(_drawn_inputs(seed))
    spreads = {'L0_conv_qkv_b': (0.0, 0.1),
     'L0_conv_proj_b': (0.0, 0.1),
     'L0_conv_mlp_b1': (0.0, 0.8),
     'L0_conv_mlp_b2': (0.0, 2.0)}
    factors = {'L0_conv_mlp_w1': 7.491, 'L0_conv_mlp_w2': 8.0, 'L0_ffn_b1': 36.842, 'L0_ffn_b2': 64.0}
    for name, (base, spread) in spreads.items():
        noise = np.random.default_rng([zlib.crc32(name.encode()), seed]).standard_normal(out[name].shape)
        drawn = base * np.exp(spread * noise) if base else spread * noise
        out[name] = jnp.asarray(drawn.astype(out[name].dtype))
    for name, factor in factors.items():
        out[name] = (out[name] * factor).astype(out[name].dtype)
    return out
```

```python
from contextlib import ExitStack

import concourse.bass as bass
from concourse import mybir

F32 = mybir.dt.float32
F16 = mybir.dt.float16
BF16 = mybir.dt.bfloat16
I32 = mybir.dt.int32
ALU = mybir.AluOpType
ACT = mybir.ActivationFunctionType
AX_X = mybir.AxisListType.X
ABSMAX = bass.bass_isa.ReduceOp.absmax

P = 128
B, C, HT, WD = 8, 384, 32, 32
N = HT * WD
KC = C // P
HEADS = 8
D = C // HEADS
PAIRS = HEADS // 2
NT = N // P
RT = P // WD
HALF = 512
MLP = max(32, C // 2)
MH = MLP // 2
FF = 4 * C
FK = FF // P
QB, QEPS = 128.0, 1e-5
CLIP = QB - QEPS
GROUPS = 5
FB = (B // GROUPS) * GROUPS
G1, G2 = FF // GROUPS, C // GROUPS
WS = 16.0
SCALE = D ** -0.5 / (WS * WS)
CS = 2048.0
NR, ND, NDP = HT + NT * RT - RT, 2 * HT - 1, 2 * HT
Z = 6
RING = 3
MX_AT = [0, 0, 3, 3, 3, 3, 4, 0]

MX_FROM = next(j for j, m in enumerate(MX_AT) if m)


def ring_plan(names):
    uses, place = [0] * RING, {}
    for n, name in enumerate(names):
        place[name] = (n % RING, uses[n % RING])
        uses[n % RING] += 1
    return place, uses


def pair_tiles(p):
    out, m = [], 0
    for j in range(NT):
        step = [("s", p, hh, j) for hh in range(2)]
        if p + 1 < PAIRS:
            step += [("m", p + 1, (m + i) // NT, (m + i) % NT) for i in range(MX_AT[j])]
            m += MX_AT[j]
            if j == NT - 2:
                step += [("ct", p + 1)]
        if p > 0 and j == 1:
            step += [("ot", p - 1)]
        if p > 0 and j == 2:
            step += [("rb", p - 1)]
        out.append(step)
    return out


ATT_TILES = (
    [("mean",), ("var",), ("rstd",)]
    + [("qk", t) for t in range(2 * KC)]
    + [("v", t) for t in range(NT // 2)]
    + [("m", 0, hh, i) for hh in range(2) for i in range(NT)]
    + [("ct", 0)]
    + [t for p in range(PAIRS) for step in pair_tiles(p) for t in step]
    + [("ot", PAIRS - 1), ("rb", PAIRS - 1)]
    + [("proj", m) for m in range(KC)]
)
FFN_TILES = [("mean",), ("var",), ("rstd",)] + [("f1", o) for o in range(FK)] + [("f2", m) for m in range(KC)]


def metaformer(nc, x, qkv_w, qkv_b, proj_w, proj_b, mlp_w1, mlp_b1, mlp_w2, mlp_b2, W1, b1, W2, b2, out):
    x_v = x.rearrange("b (k p) h w -> b p k (h w)", p=P)
    out_v = out.rearrange("b (k p) h w -> b p k (h w)", p=P)
    tab = nc.dram_tensor("tab", (HEADS, ND, NDP), F32, kind="Internal").ap()
    tabr = nc.dram_tensor("tabr", (HEADS, ND, NDP), BF16, kind="Internal").ap()
    win = nc.dram_tensor("win", (WD, HEADS, ND, WD), F32, kind="Internal").ap()
    winr = nc.dram_tensor("winr", (WD, HEADS, ND, WD), BF16, kind="Internal").ap()
    ur_d = nc.dram_tensor("ur_d", (P, HEADS, NR * WD), BF16, kind="Internal").ap()
    qk_d = nc.dram_tensor("qk_d", (B, 2, 2 * C, N), F16, kind="Internal").ap()

    with ExitStack() as top:
        def sbuf(ctx, name, shape, dt=F32):
            return ctx.enter_context(nc.sbuf_tensor(name, shape, dt))

        ident = sbuf(top, "ident", [P, P])
        mean_w = sbuf(top, "mean_w", [P, P])
        ring = [top.enter_context(nc.psum_tensor(f"ring{i}", [P, 2 * HALF], F32)) for i in range(RING)]
        acc = top.enter_context(nc.psum_tensor("acc", [P, 2 * HALF], F32))

        with ExitStack() as att:
            T = {
                "bias": sbuf(att, "bias", [P, HEADS, NR * WD]),
                "wh": sbuf(att, "wh", [P, KC, 3 * C], F16),
                "wl": sbuf(att, "wl", [P, KC, 3 * C], F16),
                "wp": sbuf(att, "wp", [P, PAIRS, C]),
                "qkb": sbuf(att, "qkb", [P, 2 * KC]),
                "pb": sbuf(att, "pb", [P, KC]),
            }
            with ExitStack() as ctx:
                setup_attention(nc, ctx, sbuf, T, ident, mean_w, ring, qkv_w, qkv_b, proj_w, proj_b,
                                mlp_w1, mlp_b1, mlp_w2, mlp_b2, tab, tabr, win, winr, ur_d)
            with ExitStack() as ctx:
                attention(nc, ctx, sbuf, T, ident, mean_w, ring, acc, x_v, out_v, ur_d, qk_d)
        with ExitStack() as ffn:
            T = {
                "w1t": sbuf(ffn, "w1t", [P, KC, FF], F16),
                "w2t": sbuf(ffn, "w2t", [P, FK, C], F16),
                "b1s": sbuf(ffn, "b1s", [P, FK]),
                "b2s": sbuf(ffn, "b2s", [P, KC]),
            }
            with ExitStack() as ctx:
                setup_ffn(nc, ctx, sbuf, T, ident, mean_w, ring, acc, W1, b1, W2, b2)
            with ExitStack() as ctx:
                feed_forward(nc, ctx, sbuf, T, ident, mean_w, ring, out_v)


def setup_attention(nc, ctx, sbuf, T, ident, mean_w, ring, qkv_w, qkv_b, proj_w, proj_b,
                    mlp_w1, mlp_b1, mlp_w2, mlp_b2, tab, tabr, win, winr, ur_d):
    def sem(name):
        return ctx.enter_context(nc.semaphore(name))

    CH = ND * NDP // 8
    wtmp = sbuf(ctx, "wtmp", [P, KC, 3 * C])
    bv = sbuf(ctx, "bv", [P, PAIRS])
    pb0 = sbuf(ctx, "pb0", [P, KC])
    w1r = [sbuf(ctx, f"w1r{i}", [1, MLP]) for i in range(2)]
    b1c = sbuf(ctx, "b1c", [MH, 2])
    w2c = sbuf(ctx, "w2c", [MH, 2, HEADS])
    b2c = sbuf(ctx, "b2c", [HEADS, 1])
    grid = sbuf(ctx, "grid", [1, 2, ND * NDP])
    hid = sbuf(ctx, "hid", [MH, 2, 2, CH])
    tab_s = sbuf(ctx, "tab_s", [HEADS, ND * NDP])
    tabr_s = sbuf(ctx, "tabr_s", [HEADS, ND * NDP], BF16)
    loads, wload, cst, pads, gridi, gridf = (sem(n) for n in ("loads", "wload", "cst", "pads", "gridi", "gridf"))
    wh_ready, hidp, hidr, tabp, tabf = (sem(n) for n in ("wh_ready", "hidp", "hidr", "tabp", "tabf"))
    tab_out, win_in, win_out, pbp, wdone = (sem(n) for n in ("tab_out", "win_in", "win_out", "pbp", "wdone"))
    block = ctx.enter_context(nc.Block())

    @block.sync
    def _(sp):
        sp.dma_start(wtmp[:, :, :], qkv_w.rearrange("(k p) n -> p k n", p=P)).then_inc(wload, 16)
        with nc.allow_non_contiguous_dma(reason="biases by partition"):
            for i in range(2):
                sp.dma_start(w1r[i][:, :], mlp_w1[i:i + 1, :]).then_inc(loads, 16)
            sp.dma_start(b1c[:, :], mlp_b1.rearrange("(a p) -> p a", a=2)).then_inc(loads, 16)
            sp.dma_start(w2c[:, :, :], mlp_w2.rearrange("(a p) n -> p a n", a=2)).then_inc(loads, 16)
            sp.dma_start(b2c[:, :], mlp_b2.rearrange("(p a) -> p a", a=1)).then_inc(loads, 16)
            sp.dma_start(T["qkb"][:, :], qkv_b[0:2 * C].rearrange("(k p) -> p k", p=P)).then_inc(loads, 16)
            sp.dma_start(pb0[:, :], proj_b.rearrange("(k p) -> p k", p=P)).then_inc(loads, 16)
            sp.wait_ge(pads, 2)
            for t in range(2):
                sp.dma_start(T["wp"][64 * t:64 * t + D, :, :],
                             proj_w.rearrange("(p t d) n -> t d p n", t=2, d=D)[t]).then_inc(loads, 16)
                sp.dma_start(bv[64 * t:64 * t + D, :],
                             qkv_b[2 * C:3 * C].rearrange("(p t d) -> t d p", t=2, d=D)[t]).then_inc(loads, 16)
        sp.wait_ge(tabf, 16)
        sp.dma_start(tab, tab_s[:, :].rearrange("h (a c) -> h a c", c=NDP)).then_inc(tab_out, 16)
        sp.dma_start(tabr, tabr_s[:, :].rearrange("h (a c) -> h a c", c=NDP)).then_inc(tab_out, 16)
        sp.wait_ge(tab_out, 32)
        for c in range(WD):
            sp.dma_start(win[c], tab[:, :, WD - 1 - c:2 * WD - 1 - c]).then_inc(win_in, 16)
        sp.wait_ge(win_in, 32 * WD)
        for r in range(RT):
            rows = slice(RT - 1 - r, RT - 1 - r + NR)
            sp.dma_start(T["bias"][r * WD:(r + 1) * WD, :, :],
                         win[:, :, rows, :].rearrange("c h a w -> c h (a w)")).then_inc(win_out, 16)
            sp.dma_start(ur_d[r * WD:(r + 1) * WD, :, :],
                         winr[:, :, rows, :].rearrange("c h a w -> c h (a w)")).then_inc(win_out, 16)
        sp.wait_ge(win_out, 32 * RT)

    @block.gpsimd
    def _(pool):
        nc.gpsimd.memset(T["wp"][:, :, :], 0.0).then_inc(pads, 1)
        nc.gpsimd.memset(bv[:, :], 0.0).then_inc(pads, 1)
        nc.gpsimd.iota(grid[0:1, 0, :], [[1, ND], [0, NDP]], base=-(HT - 1), channel_multiplier=0,
                       allow_small_or_imprecise_dtypes=True).then_inc(gridi, 1)
        nc.gpsimd.iota(grid[0:1, 1, :], [[0, ND], [1, NDP]], base=-(WD - 1), channel_multiplier=0,
                       allow_small_or_imprecise_dtypes=True).then_inc(gridi, 1)
        nc.gpsimd.memset(mean_w[:, :], 1.0 / C).then_inc(cst, 1)
        nc.gpsimd.memset(ident[:, :], 0.0).then_inc(cst, 1)
        pool.wait_ge(cst, 2)
        nc.gpsimd.affine_select(out=ident[:, :], in_=ident[:, :], compare_op=ALU.not_equal, fill=1.0, base=0,
                                pattern=[[-1, P]], channel_multiplier=1).then_inc(cst, 1)

    @block.scalar
    def _(act):
        act.wait_ge(wload, 16)
        for k in range(KC):
            nc.scalar.activation(T["wh"][:, k, :], wtmp[:, k, :], ACT.Copy, scale=WS).then_inc(wh_ready, 1)
        act.wait_ge(loads, 16 * 11)
        for c in range(8):
            act.wait_ge(hidp, c + 1)
            if c >= 1:
                act.wait_ge(tabp, c)
            for s in range(2):
                for a in range(2):
                    nc.scalar.activation(hid[:, s, a, :], ring[c % 2][0:MH, a * HALF:a * HALF + CH], ACT.Gelu,
                                         bias=b1c[:, a:a + 1], scale=1.0 - 2.0 * s).then_inc(hidr, 1)
        act.wait_ge(tab_out, 32)
        for c in range(WD):
            act.dma_start(winr[c], tabr[:, :, WD - 1 - c:2 * WD - 1 - c]).then_inc(win_in, 16)

    @block.tensor
    def _(pe):
        pe.wait_ge(loads, 16 * 11)
        pe.wait_ge(gridf, 2)
        for c in range(8):
            if c >= 2:
                pe.wait_ge(hidr, 4 * (c - 1))
            for a in range(2):
                for i in range(2):
                    last = nc.tensor.matmul(ring[c % 2][0:MH, a * HALF:a * HALF + CH],
                                            w1r[i][0:1, a * MH:(a + 1) * MH], grid[0:1, i, c * CH:(c + 1) * CH],
                                            start=i == 0, stop=i == 1)
            last.then_inc(hidp, 1)
            pe.wait_ge(hidr, 4 * (c + 1))
            if c >= 1:
                pe.wait_ge(tabf, 2 * c)
            for s in range(2):
                for a in range(2):
                    last = nc.tensor.matmul(ring[2][0:HEADS, s * HALF:s * HALF + CH], w2c[:, a, :],
                                            hid[:, s, a, :], start=a == 0, stop=a == 1)
            last.then_inc(tabp, 1)
        pe.wait_ge(tabf, 16)
        for m in range(KC):
            for p in range(PAIRS):
                last = nc.tensor.matmul(ring[2][:, m:m + 1], T["wp"][:, p, m * P:(m + 1) * P], bv[:, p:p + 1],
                                        start=p == 0, stop=p == PAIRS - 1)
        last.then_inc(pbp, 1)

    @block.vector
    def _(dve):
        dve.wait_ge(gridi, 2)
        for i in range(2):
            nc.vector.tensor_scalar(grid[0:1, i, :], grid[0:1, i, :], 1.0 / (HT - 1), None, ALU.mult).then_inc(gridf, 1)
        for k in range(KC):
            dve.wait_ge(wh_ready, k + 1)
            nc.vector.scalar_tensor_tensor(out=T["wl"][:, k, :], in0=wtmp[:, k, :], scalar=WS, in1=T["wh"][:, k, :],
                                           op0=ALU.mult, op1=ALU.subtract).then_inc(wdone, 1)
        dve.wait_ge(loads, 16 * 11)
        nc.vector.tensor_scalar(T["qkb"][:, :], T["qkb"][:, :], WS, None, ALU.mult).then_inc(wdone, 1)
        for c in range(8):
            dve.wait_ge(tabp, c + 1)
            cols = slice(c * CH, (c + 1) * CH)
            nc.vector.tensor_scalar(tab_s[:, cols], ring[2][0:HEADS, 0:CH], b2c[:, 0:1], None, ALU.add).then_inc(tabf, 1)
            nc.vector.tensor_scalar(tabr_s[:, cols], ring[2][0:HEADS, HALF:HALF + CH], b2c[:, 0:1], 1.0 / SCALE,
                                    ALU.add, ALU.mult).then_inc(tabf, 1)
        dve.wait_ge(pbp, 1)
        nc.vector.tensor_tensor(T["pb"][:, :], ring[2][:, 0:KC], pb0[:, :], ALU.add).then_inc(wdone, 1)


def attention(nc, ctx, sbuf, T, ident, mean_w, ring, acc, x_v, out_v, ur_d, qk_d):
    def sem(name):
        return ctx.enter_context(nc.semaphore(name))

    place, uses = ring_plan(ATT_TILES)
    bias, wh, wl, wp, qkb, pb = (T[k] for k in ("bias", "wh", "wl", "wp", "qkb", "pb"))
    xo = sbuf(ctx, "xo", [P, PAIRS, N])
    xn = sbuf(ctx, "xn", [P, 2, KC, N], F16)
    res = xn[:, :, :, :].rearrange("p s k n -> p (s k n)").bitcast(F32).rearrange("p (k n) -> p k n", n=N)
    st = sbuf(ctx, "st", [P, 2, 2, N], F16)
    q2 = sbuf(ctx, "q2", [P, 2, 2, N], F16)
    kh = sbuf(ctx, "kh", [P, 2, 2, N], F16)
    kl = sbuf(ctx, "kl", [P, 2, 2, N], F16)
    ur = sbuf(ctx, "ur", [P, 2, 2, NR * WD], BF16)
    v = sbuf(ctx, "v", [P, NT, HEADS, 64])
    zp = sbuf(ctx, "zp", [P, Z, N])
    osb = sbuf(ctx, "osb", [P, N])
    cm = sbuf(ctx, "cm", [P, 2, 2 * NT])
    ct = sbuf(ctx, "ct", [2 * NT, 2, P], F16)
    rc = sbuf(ctx, "rc", [P, NT, 2])
    std = sbuf(ctx, "std", [P, NT])
    rstd = sbuf(ctx, "rstd", [P, NT])
    eps = sbuf(ctx, "eps", [P, 1])

    ready = [sem(f"ready{i}") for i in range(RING)]
    free = [sem(f"free{i}") for i in range(RING)]
    names = ("consts", "x_in", "xc_ready", "sq_ready", "rstd_ready", "xn_ready", "xh_ready",
             "xl_ready", "sh_ready", "res_in", "p_ready", "pv_done", "osb_ready",
             "stored", "step", "image")
    S = {n: sem(n) for n in names}
    st_out = [sem(f"st_out{i}") for i in range(2)]
    qk_in = [sem(f"qk_in{i}") for i in range(2)]
    max_in = [sem(f"max_in{i}") for i in range(2)]
    block = ctx.enter_context(nc.Block())
    QK_DMAS, NTILE = 13, PAIRS * NT * 2

    def taken(eng, tile, b):
        slot, n = place[tile]
        eng.wait_ge(free[slot], b * uses[slot] + n + 1)
        return ring[slot], ready[slot]

    def filled(eng, tile, b):
        slot, n = place[tile]
        eng.wait_ge(ready[slot], b * uses[slot] + n + 1)
        return ring[slot], free[slot]

    def read(eng, tile, b, into=None):
        slot, n = place[tile]
        if into is not None and place[into][0] == slot:
            return
        eng.wait_ge(free[slot], b * uses[slot] + n + 2)

    def load_pair(sp, p, b):
        i = p % 2
        if p >= 2:
            filled(sp, ("s", p - 2, 1, NT - 1), b)
        for hh in range(2):
            h = 2 * p + hh
            for s in range(2):
                q = qk_d[bass.ds(b, 1), s, h * D:(h + 1) * D, :].squeeze(0)
                sp.dma_start(q2[s * D:(s + 1) * D, i, hh, :], q).then_inc(qk_in[i], 16)
                for part, dst in ((0, kh), (1, kl)):
                    k = qk_d[bass.ds(b, 1), part, C + h * D:C + (h + 1) * D, :].squeeze(0)
                    sp.dma_start(dst[s * D:(s + 1) * D, i, hh, :], k).then_inc(qk_in[i], 16)
        sp.dma_start(ur[:, i, :, :], ur_d[:, 2 * p:2 * p + 2, :]).then_inc(qk_in[i], 16)

    def max_rows(sp, p, b):
        read(sp, ("ct", p), b)
        for hh in range(2):
            sp.dma_start(q2[2 * D:2 * D + 1, p % 2, hh, :],
                         ct[hh * NT:(hh + 1) * NT, p % 2, :]).then_inc(max_in[p % 2], 16)

    @block.sync
    def _(sp):
        with sp.Fori(0, B) as b:
            sp.dma_start(xo[:, 0:KC, :], x_v[bass.ds(b, 1)].squeeze(0)).then_inc(S["x_in"], 16)
            for t in range(2 * KC):
                read(sp, ("qk", t), b)
                for s in range(2):
                    sp.dma_start(qk_d[bass.ds(b, 1), s, t * P:(t + 1) * P, :].squeeze(0),
                                 st[:, t % 2, s, :]).then_inc(st_out[t % 2], 16)
            filled(sp, ("v", NT // 2 - 1), b)
            sp.dma_start(res, x_v[bass.ds(b, 1)].squeeze(0)).then_inc(S["res_in"], 16)
            for i in range(2):
                sp.wait_ge(st_out[i], b * (32 * KC) + 32 * KC)
            for p in range(PAIRS):
                i = p % 2
                if p >= 1:
                    max_rows(sp, p, b)
                if p == 0:
                    load_pair(sp, 0, b)
                    load_pair(sp, 1, b)
                    max_rows(sp, 0, b)
                if 2 <= p + 1 < PAIRS:
                    load_pair(sp, p + 1, b)
            read(sp, ("proj", KC - 1), b)
            sp.dma_start(out_v[bass.ds(b, 1)].squeeze(0), res).then_inc(S["stored"], 16)
            sp.wait_ge(S["stored"], b * 16 + 16)
            sp.sem_inc(S["image"], 1)
        sp.wait_ge(S["stored"], 16 * B)

    @block.gpsimd
    def _(pool):
        nc.gpsimd.memset(v[:, :, :, :], 1.0).then_inc(S["consts"], 1)
        pool.wait_ge(S["consts"], 1)
        nc.gpsimd.memset(kh[2 * D:P, :, :, :], CS).then_inc(S["consts"], 1)
        pool.wait_ge(S["consts"], 2)
        nc.gpsimd.memset(eps[:, :], 1e-6).then_inc(S["consts"], 1)

    @block.tensor
    def _(pe):
        def scores(p, hh, j, b):
            buf, done = taken(pe, ("s", p, hh, j), b)
            i = p % 2
            for f in range(2):
                cols = slice(f * HALF, (f + 1) * HALF)
                nc.tensor.matmul(buf[:, cols], kh[0:2 * D + 1, i, hh, j * P:(j + 1) * P],
                                 q2[0:2 * D + 1, i, hh, cols], start=True, stop=False)
                last = nc.tensor.matmul(buf[:, cols], kl[0:2 * D, i, hh, j * P:(j + 1) * P],
                                        q2[0:2 * D, i, hh, cols], start=False, stop=True)
            last.then_inc(done, 1)

        def max_scores(p, hh, i, b):
            buf, done = taken(pe, ("m", p, hh, i), b)
            for f in range(2):
                cols = slice(f * HALF, (f + 1) * HALF)
                last = nc.tensor.matmul(buf[:, cols], q2[0:2 * D, p % 2, hh, i * P:(i + 1) * P],
                                        kh[0:2 * D, p % 2, hh, cols], start=True, stop=True)
            last.then_inc(done, 1)

        def max_transpose(p, b):
            buf, done = taken(pe, ("ct", p), b)
            read(pe, ("m", p, 1, NT - 1), b, ("ct", p))
            nc.tensor.transpose(buf[0:2 * NT, 0:P], cm[:, p % 2, :], ident[:, :]).then_inc(done, 1)

        def values(p, j, b):
            k = 2 * NT * p + 2 * j
            pe.wait_ge(S["p_ready"], b * NTILE + k + 2)
            if j == 0 and p >= 1:
                pe.wait_ge(S["osb_ready"], b * PAIRS + p)
            for f in range(2):
                cols = slice(f * HALF, (f + 1) * HALF)
                for hh in range(2):
                    last = nc.tensor.matmul(acc[64 * hh:64 * hh + 64, cols], v[:, j, 2 * p + hh, :],
                                            zp[:, (k + hh) % Z, cols], start=j == 0, stop=j == NT - 1)
            last.then_inc(S["pv_done"], 2)

        def sums_transpose(p, b):
            buf, done = taken(pe, ("ot", p), b)
            pe.wait_ge(S["osb_ready"], b * PAIRS + p + 1)
            for i in range(NT):
                last = nc.tensor.transpose(buf[:, i * P:(i + 1) * P], osb[:, i * P:(i + 1) * P], ident[:, :])
            last.then_inc(done, 1)

        def sums_broadcast(p, b):
            buf, done = taken(pe, ("rb", p), b)
            read(pe, ("ot", p), b, ("rb", p))
            for i in range(NT):
                for hh in range(2):
                    last = nc.tensor.matmul(buf[64 * hh:64 * hh + 64, i * P:(i + 1) * P],
                                            rc[:, i, hh:hh + 1].to_broadcast([P, 64]), ident[:, :],
                                            start=True, stop=True)
            last.then_inc(done, 1)

        pe.wait_ge(S["consts"], 3)
        with pe.Fori(0, B) as b:
            pe.wait_ge(S["x_in"], b * 16 + 16)
            layernorm_pe(nc, pe, taken, b, S, xo, zp, mean_w, ident, rstd)
            pe.wait_ge(S["xl_ready"], b * KC + KC)
            terms = [(w, s, k) for w, s in ((wh, 0), (wh, 1), (wl, 0)) for k in range(KC)]
            for t in range(2 * KC):
                buf, done = taken(pe, ("qk", t), b)
                for f in range(2):
                    cols = slice(f * HALF, (f + 1) * HALF)
                    for n, (w, s, k) in enumerate(terms):
                        last = nc.tensor.matmul(buf[:, cols], w[:, k, t * P:(t + 1) * P], xn[:, s, k, cols],
                                                start=n == 0, stop=n == len(terms) - 1)
                last.then_inc(done, 1)
            for t in range(NT // 2):
                buf, done = taken(pe, ("v", t), b)
                for f in range(2):
                    rows = slice((2 * t + f) * P, (2 * t + f + 1) * P)
                    for n, (w, s, k) in enumerate(terms):
                        last = nc.tensor.matmul(buf[:, f * HALF:f * HALF + C], xn[:, s, k, rows], w[:, k, 2 * C:3 * C],
                                                start=n == 0, stop=n == len(terms) - 1)
                last.then_inc(done, 1)
            pe.wait_ge(qk_in[0], b * (2 * 16 * QK_DMAS) + 16 * QK_DMAS)
            for hh in range(2):
                for i in range(NT):
                    max_scores(0, hh, i, b)
            max_transpose(0, b)
            read(pe, ("v", NT // 2 - 1), b, ("s", 0, 0, 0))
            for p in range(PAIRS):
                pe.wait_ge(max_in[p % 2], b * 64 + 32 * (p // 2 + 1))
                for j, step in enumerate(pair_tiles(p)):
                    if p + 1 < PAIRS and j == MX_FROM:
                        pe.wait_ge(qk_in[(p + 1) % 2], b * (2 * 16 * QK_DMAS) + 16 * QK_DMAS * ((p + 1) // 2 + 1))
                    for kind, *at in step:
                        if kind == "s":
                            scores(*at, b)
                        elif kind == "m":
                            max_scores(*at, b)
                        elif kind == "ct":
                            max_transpose(*at, b)
                        elif kind == "ot":
                            sums_transpose(*at, b)
                        else:
                            sums_broadcast(*at, b)
                    if j >= 1:
                        values(p, j - 1, b)
                values(p, NT - 1, b)
            sums_transpose(PAIRS - 1, b)
            sums_broadcast(PAIRS - 1, b)
            read(pe, ("rb", PAIRS - 1), b, ("proj", 0))
            for m in range(KC):
                buf, done = taken(pe, ("proj", m), b)
                for f in range(2):
                    cols = slice(f * HALF, (f + 1) * HALF)
                    for p in range(PAIRS):
                        last = nc.tensor.matmul(buf[:, cols], wp[:, p, m * P:(m + 1) * P], xo[:, p, cols],
                                                start=p == 0, stop=p == PAIRS - 1)
                last.then_inc(done, 1)

    @block.scalar
    def _(act):
        def exps(p, j, b):
            for hh in range(2):
                k = 2 * NT * p + 2 * j + hh
                read(act, ("s", p, hh, j), b)
                nc.scalar.activation(zp[:, k % Z, :], zp[:, k % Z, :], ACT.Exp).then_inc(S["p_ready"], 1)

        def max_evac(p, b):
            buf, done = filled(act, ("ct", p), b)
            nc.scalar.activation(ct[:, p % 2, :], buf[0:2 * NT, 0:P], ACT.Copy, scale=-1.0 / CS).then_inc(done, 1)

        for f in free:
            act.sem_inc(f, 1)
        act.wait_ge(S["consts"], 3)
        with act.Fori(0, B) as b:
            layernorm_act(nc, act, filled, read, b, S, xo, zp, std, eps, xn)
            for t in range(2 * KC):
                buf, _done = filled(act, ("qk", t), b)
                if t >= 2:
                    act.wait_ge(st_out[t % 2], b * (32 * KC) + 32 * (t // 2))
                nc.scalar.activation(st[:, t % 2, 0, :], buf[:, :], ACT.Identity, bias=qkb[:, t:t + 1])\
                    .then_inc(S["sh_ready"], 1)
            for t in range(NT // 2):
                buf, done = filled(act, ("v", t), b)
                for f in range(2):
                    last = nc.scalar.activation(
                        v[:, 2 * t + f, :, 0:D],
                        buf[:, f * HALF:f * HALF + C].rearrange("p (h d) -> p h d", d=D), ACT.Copy, scale=1.0 / WS)
                last.then_inc(done, 1)
            max_evac(0, b)
            for p in range(PAIRS):
                for j in range(NT):
                    exps(p, j, b)
                    if j == NT - 3 and p + 1 < PAIRS:
                        max_evac(p + 1, b)
                act.wait_ge(S["pv_done"], b * NTILE + 2 * NT * (p + 1))
                if p >= 1:
                    read(act, ("rb", p - 1), b)
                nc.scalar.activation(osb[:, :], acc[:, :], ACT.Copy).then_inc(S["osb_ready"], 1)

    @block.vector
    def _(dve):
        def softmax_in(p, hh, j, b):
            buf, done = filled(dve, ("s", p, hh, j), b)
            k = 2 * NT * p + 2 * j + hh
            if k >= Z:
                dve.wait_ge(S["pv_done"], b * NTILE + k - Z + 1)
            at = (NT - 1 - j) * RT * WD
            i = nc.vector.scalar_tensor_tensor(out=zp[:, k % Z, :], in0=buf[:, :], scalar=SCALE,
                                               in1=bias[:, 2 * p + hh, at:at + N], op0=ALU.mult, op1=ALU.add)
            i.then_inc(done, 1)

        def row_max(p, hh, i, b):
            buf, done = filled(dve, ("m", p, hh, i), b)
            at = (NT - 1 - i) * RT * WD
            n = hh * NT + i
            dve.sem_inc(S["step"], 1)
            r = nc.vector.tensor_tensor_reduce(out=buf[:, :], in0=buf[:, :], in1=ur[:, p % 2, hh, at:at + N],
                                               scale=1.0, scalar=-3.0e38, op0=ALU.add, op1=ALU.max,
                                               accum_out=cm[:, p % 2, n:n + 1])
            r.then_inc(done, 1)

        def sums_inverse(p, b):
            buf, done = filled(dve, ("ot", p), b)
            r = nc.vector.reciprocal(rc[:, :, :], buf[:, :].rearrange("p (i c) -> p i c", c=P)[:, :, D:D + 65:64])
            r.then_inc(done, 1)

        def normalise(p, b):
            buf, done = filled(dve, ("rb", p), b)
            r = nc.vector.tensor_tensor(xo[:, p, :], osb[:, :], buf[:, :], ALU.mult)
            r.then_inc(done, 1)

        with dve.Fori(0, B) as b:
            layernorm_dve(nc, dve, filled, read, b, S, xo, std, rstd, xn, xo)
            for t in range(2 * KC):
                dve.wait_ge(S["sh_ready"], b * (2 * KC) + t + 1)
                buf, done = filled(dve, ("qk", t), b)
                r = nc.vector.scalar_tensor_tensor(out=st[:, t % 2, 1, :], in0=buf[:, :], scalar=qkb[:, t:t + 1],
                                                   in1=st[:, t % 2, 0, :], op0=ALU.add, op1=ALU.subtract)
                r.then_inc(done, 1)
            dve.wait_ge(qk_in[0], b * (2 * 16 * QK_DMAS) + 16 * QK_DMAS)
            for hh in range(2):
                for i in range(NT):
                    row_max(0, hh, i, b)
            for p in range(PAIRS):
                for j, step in enumerate(pair_tiles(p)):
                    if p + 1 < PAIRS and j == MX_FROM:
                        dve.wait_ge(qk_in[(p + 1) % 2], b * (2 * 16 * QK_DMAS) + 16 * QK_DMAS * ((p + 1) // 2 + 1))
                    for kind, *at in step:
                        if kind == "s":
                            softmax_in(*at, b)
                        elif kind == "m":
                            row_max(*at, b)
                        elif kind == "ot":
                            sums_inverse(*at, b)
                        elif kind == "rb":
                            normalise(*at, b)
            sums_inverse(PAIRS - 1, b)
            normalise(PAIRS - 1, b)
            dve.wait_ge(S["res_in"], b * 16 + 16)
            for m in range(KC):
                buf, done = filled(dve, ("proj", m), b)
                r = nc.vector.scalar_tensor_tensor(out=res[:, m, :], in0=buf[:, :], scalar=pb[:, m:m + 1],
                                                   in1=res[:, m, :], op0=ALU.add, op1=ALU.add)
                r.then_inc(done, 1)


def layernorm_pe(nc, pe, taken, b, S, xc, sq, mean_w, ident, rstd):
    buf, done = taken(pe, ("mean",), b)
    for f in range(2):
        cols = slice(f * HALF, (f + 1) * HALF)
        for k in range(KC):
            last = nc.tensor.matmul(buf[:, cols], mean_w[:, :], xc[:, k, cols], start=k == 0, stop=k == KC - 1)
    last.then_inc(done, 1)
    buf, done = taken(pe, ("var",), b)
    pe.wait_ge(S["sq_ready"], b * KC + KC)
    for i in range(NT):
        for k in range(KC):
            last = nc.tensor.matmul(buf[:, i:i + 1], sq[:, k, i * P:(i + 1) * P], mean_w[:, 0:1],
                                    start=k == 0, stop=k == KC - 1)
    last.then_inc(done, 1)
    buf, done = taken(pe, ("rstd",), b)
    pe.wait_ge(S["rstd_ready"], b + 1)
    for i in range(NT):
        last = nc.tensor.matmul(buf[:, i * P:(i + 1) * P], rstd[:, i:i + 1].to_broadcast([P, P]), ident[:, :],
                                start=True, stop=True)
    last.then_inc(done, 1)


def layernorm_act(nc, act, filled, read, b, S, xc, sq, std, eps, xn):
    for k in range(KC):
        if k < KC - 1:
            act.wait_ge(S["xc_ready"], b * (KC - 1) + k + 1)
        else:
            read(act, ("mean",), b)
        nc.scalar.activation(sq[:, k, :], xc[:, k, :], ACT.Square).then_inc(S["sq_ready"], 1)
    buf, done = filled(act, ("var",), b)
    r = nc.scalar.activation(std[:, :], buf[:, 0:NT], ACT.Sqrt, bias=eps[:, 0:1])
    r.then_inc(done, 1)
    for k in range(KC):
        if k < KC - 1:
            act.wait_ge(S["xn_ready"], b * (KC - 1) + k + 1)
        else:
            read(act, ("rstd",), b)
        nc.scalar.activation(xn[:, 0, k, :], xc[:, k, :], ACT.Copy).then_inc(S["xh_ready"], 1)


def layernorm_dve(nc, dve, filled, read, b, S, src, std, rstd, xn, xc):
    buf, done = filled(dve, ("mean",), b)
    for k in range(KC):
        nc.vector.tensor_tensor(xc[:, k, :], src[:, k, :], buf[:, :], ALU.subtract)\
            .then_inc(S["xc_ready"] if k < KC - 1 else done, 1)
    read(dve, ("var",), b)
    nc.vector.reciprocal(rstd[:, :], std[:, :]).then_inc(S["rstd_ready"], 1)
    buf, done = filled(dve, ("rstd",), b)
    dve.wait_ge(S["sq_ready"], b * KC + KC)
    for k in range(KC):
        nc.vector.tensor_tensor(xc[:, k, :], xc[:, k, :], buf[:, :], ALU.mult)\
            .then_inc(S["xn_ready"] if k < KC - 1 else done, 1)
    for k in range(KC):
        dve.wait_ge(S["xh_ready"], b * KC + k + 1)
        nc.vector.tensor_tensor(xn[:, 1, k, :], xc[:, k, :], xn[:, 0, k, :], ALU.subtract).then_inc(S["xl_ready"], 1)


def setup_ffn(nc, ctx, sbuf, T, ident, mean_w, ring, acc, W1, b1, W2, b2):
    def sem(name):
        return ctx.enter_context(nc.semaphore(name))

    mats = ((W1, FK, C, G1, T["w1t"]), (W2, KC, FF, G2, T["w2t"]))
    w = [sbuf(ctx, f"w{i}", [P, m[1], m[2]]) for i, m in enumerate(mats)]
    sg = [sbuf(ctx, f"sg{i}", [P, m[1], m[2]], F16) for i, m in enumerate(mats)]
    mask = [sbuf(ctx, f"mask{i}", [P, m[1], GROUPS]) for i, m in enumerate(mats)]
    prod = [sbuf(ctx, f"prod{i}", [P, m[1], GROUPS]) for i, m in enumerate(mats)]
    rs = [sbuf(ctx, f"rs{i}", [P, m[1]]) for i, m in enumerate(mats)]
    gs = [sbuf(ctx, f"gs{i}", [P, GROUPS]) for i, m in enumerate(mats)]
    gm = [sbuf(ctx, f"gm{i}", [P, GROUPS]) for i, m in enumerate(mats)]
    rm = [sbuf(ctx, f"rm{i}", [P, m[1]]) for i, m in enumerate(mats)]
    live = [sbuf(ctx, f"live{i}", [P, m[1]]) for i, m in enumerate(mats)]
    idh = sbuf(ctx, "idh", [P, P], F16)
    w_in, b_in, masks, sums, group, chain, signs, tp, tc = (
        sem(n) for n in ("w_in", "b_in", "masks", "sums", "group", "chain", "signs", "tp", "tc"))
    block = ctx.enter_context(nc.Block())
    blocks = [(i, r, c) for i, m in enumerate(mats) for r in range(m[1]) for c in range(m[2] // P)]
    lots = [blocks[n:n + 4] for n in range(0, len(blocks), 4)]

    @block.sync
    def _(sp):
        for i, m in enumerate(mats):
            sp.dma_start(w[i][:, :, :], m[0].rearrange("(k p) n -> p k n", p=P)).then_inc(w_in, 16)
        with nc.allow_non_contiguous_dma(reason="biases by partition"):
            sp.dma_start(T["b1s"][:, :], b1.rearrange("(k p) -> p k", p=P)).then_inc(b_in, 16)
            sp.dma_start(T["b2s"][:, :], b2.rearrange("(k p) -> p k", p=P)).then_inc(b_in, 16)
        sp.wait_ge(b_in, 32)

    @block.gpsimd
    def _(pool):
        n = 0
        for i, m in enumerate(mats):
            nc.gpsimd.memset(mask[i][:, :, :], 1.0).then_inc(masks, 1)
            for base, mult in ((0, 1), (m[3] - 1, -1)):
                n += 1
                pool.wait_ge(masks, n)
                nc.gpsimd.affine_select(out=mask[i][:, :, :], in_=mask[i][:, :, :], compare_op=ALU.is_ge, fill=0.0,
                                        base=base, pattern=[[mult * P, m[1]], [-mult * m[3], GROUPS]],
                                        channel_multiplier=mult).then_inc(masks, 1)
            n += 1

    @block.scalar
    def _(act):
        nc.scalar.activation(idh[:, :], ident[:, :], ACT.Copy).then_inc(signs, 1)
        for i, m in enumerate(mats):
            act.wait_ge(chain, 6 * (i + 1))
            for r in range(m[1]):
                nc.scalar.activation(sg[i][:, r, :], w[i][:, r, :], ACT.Sign, bias=rm[i][:, r:r + 1]).then_inc(signs, 1)

    @block.vector
    def _(dve):
        dve.wait_ge(w_in, 32)
        dve.wait_ge(masks, 6)
        n = 0

        def link(ins):
            nonlocal n
            n += 1
            ins.then_inc(chain, 1)
            dve.wait_ge(chain, n)

        for i, m in enumerate(mats):
            link(nc.vector.tensor_reduce(out=rs[i][:, :], in_=w[i][:, :, :], axis=AX_X, op=ALU.add))
            link(nc.vector.tensor_tensor(prod[i][:, :, :], mask[i][:, :, :],
                                         rs[i][:, :].unsqueeze(2).to_broadcast([P, m[1], GROUPS]), ALU.mult))
            nc.vector.tensor_reduce(out=gs[i][:, :], in_=prod[i][:, :, :].rearrange("p k g -> p g k"), axis=AX_X,
                                    op=ALU.add).then_inc(sums, 1)
            dve.wait_ge(group, i + 1)
            link(nc.vector.tensor_scalar(gm[i][:, :], acc[:, HALF * i:HALF * i + GROUPS], -float(C) / (m[3] * m[2]),
                                         None, ALU.mult))
            link(nc.vector.tensor_tensor(prod[i][:, :, :], mask[i][:, :, :],
                                         gm[i][:, :].unsqueeze(1).to_broadcast([P, m[1], GROUPS]), ALU.mult))
            link(nc.vector.tensor_reduce(out=live[i][:, :], in_=mask[i][:, :, :], axis=AX_X, op=ALU.add))
            link(nc.vector.tensor_reduce(out=rm[i][:, :], in_=prod[i][:, :, :], axis=AX_X, op=ALU.add))
        done = 1
        for i, m in enumerate(mats):
            r = m[1] - 1
            done += m[1]
            dve.wait_ge(signs, done)
            nc.vector.tensor_scalar(sg[i][:, r, :], sg[i][:, r, :], live[i][:, r:r + 1], None, ALU.mult)\
                .then_inc(chain, 1)
        for q, lot in enumerate(lots):
            dve.wait_ge(tp, q + 1)
            for n, (i, r, c) in enumerate(lot):
                src = ring[q % RING][:, 0:HALF].bitcast(F16)[:, n * P:(n + 1) * P]
                last = nc.vector.tensor_copy(mats[i][4][:, c, r * P:(r + 1) * P], src)
            last.then_inc(tc, 1)

    @block.tensor
    def _(pe):
        for i in range(2):
            pe.wait_ge(sums, i + 1)
            nc.tensor.matmul(acc[:, HALF * i:HALF * i + GROUPS], mean_w[:, :], gs[i][:, :], start=True, stop=True)\
                .then_inc(group, 1)
        pe.wait_ge(signs, 1 + FK + KC)
        pe.wait_ge(chain, 14)
        for q, lot in enumerate(lots):
            if q >= RING:
                pe.wait_ge(tc, q - RING + 1)
            for n, (i, r, c) in enumerate(lot):
                last = nc.tensor.transpose(ring[q % RING][:, 0:HALF].bitcast(F16)[:, n * P:(n + 1) * P],
                                           sg[i][:, r, c * P:(c + 1) * P], idh[:, :])
            last.then_inc(tp, 1)


def feed_forward(nc, ctx, sbuf, T, ident, mean_w, ring, out_v):
    def sem(name):
        return ctx.enter_context(nc.semaphore(name))

    place, uses = ring_plan(FFN_TILES)
    w1t, w2t, b1s, b2s = (T[k] for k in ("w1t", "w2t", "b1s", "b2s"))
    t = sbuf(ctx, "t", [P, KC, N])
    xc = sbuf(ctx, "xc", [P, KC, N])
    sq = sbuf(ctx, "sq", [P, KC, N])
    xn = sbuf(ctx, "fxn", [P, 2, KC, N], F16)
    y = sbuf(ctx, "y", [P, FK, N])
    NH = 4
    h = sbuf(ctx, "h", [P, NH, 2, N], F16)
    am = sbuf(ctx, "am", [P, FK])
    am1 = sbuf(ctx, "am1", [P, 1])
    gam = sbuf(ctx, "gam", [P, 1])
    ge = sbuf(ctx, "ge", [P, 1])
    gr = sbuf(ctx, "gr", [P, 1])
    sc = sbuf(ctx, "sc", [P, 2])
    std = sbuf(ctx, "fstd", [P, NT])
    rstd = sbuf(ctx, "frstd", [P, NT])
    eps = sbuf(ctx, "feps", [P, 1])
    ready = [sem(f"fready{i}") for i in range(RING)]
    free = [sem(f"ffree{i}") for i in range(RING)]
    names = ("consts", "t_in", "xc_ready", "sq_ready", "rstd_ready", "xn_ready", "xh_ready", "xl_ready",
             "am_ready", "gam_ready", "chain", "s_ready", "g_ready", "hh_ready", "hl_ready", "h_used",
             "clipped", "t_ready", "stored", "step", "image")
    S = {n: sem("f_" + n) for n in names}
    block = ctx.enter_context(nc.Block())

    def taken(eng, tile, b):
        slot, n = place[tile]
        eng.wait_ge(free[slot], b * uses[slot] + n + 1)
        return ring[slot], ready[slot]

    def filled(eng, tile, b):
        slot, n = place[tile]
        eng.wait_ge(ready[slot], b * uses[slot] + n + 1)
        return ring[slot], free[slot]

    def read(eng, tile, b, into=None):
        slot, n = place[tile]
        if into is not None and place[into][0] == slot:
            return
        eng.wait_ge(free[slot], b * uses[slot] + n + 2)

    @block.sync
    def _(sp):
        with sp.Fori(0, FB) as b:
            sp.dma_start(t[:, :, :], out_v[bass.ds(b, 1)].squeeze(0)).then_inc(S["t_in"], 16)
            sp.wait_ge(S["t_ready"], b * KC + KC)
            sp.dma_start(out_v[bass.ds(b, 1)].squeeze(0), t[:, :, :]).then_inc(S["stored"], 16)
            sp.wait_ge(S["stored"], b * 16 + 16)
            sp.sem_inc(S["image"], 1)
        sp.wait_ge(S["stored"], 16 * FB)

    @block.gpsimd
    def _(pool):
        nc.gpsimd.memset(eps[:, :], 1e-5).then_inc(S["consts"], 1)
        with pool.Fori(0, FB) as b:
            for s in range(2):
                pool.wait_ge(S["am_ready"], b * 2 + s + 1)
                pool.sem_inc(S["step"], 1)
                nc.gpsimd.partition_all_reduce(gam[:, :], am1[:, :], P, ABSMAX).then_inc(S["gam_ready"], 1)

    @block.tensor
    def _(pe):
        pe.wait_ge(S["consts"], 1)
        with pe.Fori(0, FB) as b:
            pe.wait_ge(S["t_in"], b * 16 + 16)
            layernorm_pe(nc, pe, taken, b, S, t, sq, mean_w, ident, rstd)
            pe.wait_ge(S["xl_ready"], b * KC + KC)
            for o in range(FK):
                buf, done = taken(pe, ("f1", o), b)
                for f in range(2):
                    cols = slice(f * HALF, (f + 1) * HALF)
                    for s in range(2):
                        for k in range(KC):
                            last = nc.tensor.matmul(buf[:, cols], w1t[:, k, o * P:(o + 1) * P], xn[:, s, k, cols],
                                                    start=s == 0 and k == 0, stop=s == 1 and k == KC - 1)
                last.then_inc(done, 1)
            accs = [taken(pe, ("f2", m), b) for m in range(KC)]
            for k in range(FK):
                pe.wait_ge(S["hl_ready"], b * FK + k + 1)
                for m in range(KC):
                    for f in range(2):
                        cols = slice(f * HALF, (f + 1) * HALF)
                        for s in range(2):
                            last = nc.tensor.matmul(accs[m][0][:, cols], w2t[:, k, m * P:(m + 1) * P],
                                                    h[:, k % NH, s, cols], start=k == 0 and s == 0,
                                                    stop=k == FK - 1 and s == 1)
                    if k == FK - 1:
                        last.then_inc(accs[m][1], 1)
                if k < FK - 1:
                    last.then_inc(S["h_used"], 1)

    @block.scalar
    def _(act):
        for f in free:
            act.sem_inc(f, 1)
        act.wait_ge(S["consts"], 1)
        with act.Fori(0, FB) as b:
            layernorm_act(nc, act, filled, read, b, S, xc, sq, std, eps, xn)
            for o in range(FK):
                buf, done = filled(act, ("f1", o), b)
                r = nc.scalar.activation(y[:, o, :], buf[:, :], ACT.Identity, bias=b1s[:, o:o + 1])
                r.then_inc(done, 1)
            act.wait_ge(S["s_ready"], b * 2 + 1)
            for o in range(FK):
                nc.scalar.activation(y[:, o, :], y[:, o, :], ACT.Gelu, scale=sc[:, 0:1]).then_inc(S["g_ready"], 1)
            for m in range(KC):
                buf, done = filled(act, ("f2", m), b)
                r = nc.scalar.activation(y[:, m, :], buf[:, :], ACT.Identity, bias=b2s[:, m:m + 1])
                r.then_inc(done, 1)

    @block.vector
    def _(dve):
        def scale_of(b, s, n):
            if s >= 1:
                dve.wait_ge(S["s_ready"], b * 2 + s)
            nc.vector.tensor_reduce(out=am1[:, :], in_=am[:, 0:n], axis=AX_X, op=ALU.max).then_inc(S["am_ready"], 1)
            dve.wait_ge(S["gam_ready"], b * 2 + s + 1)
            nc.vector.tensor_scalar(ge[:, :], gam[:, :], QEPS, None, ALU.add).then_inc(S["chain"], 1)
            dve.wait_ge(S["chain"], b * 4 + 2 * s + 1)
            nc.vector.reciprocal(gr[:, :], ge[:, :]).then_inc(S["chain"], 1)
            dve.wait_ge(S["chain"], b * 4 + 2 * s + 2)
            nc.vector.tensor_scalar(sc[:, s:s + 1], gr[:, :], QB, None, ALU.mult).then_inc(S["s_ready"], 1)

        with dve.Fori(0, FB) as b:
            layernorm_dve(nc, dve, filled, read, b, S, t, std, rstd, xn, xc)
            for o in range(FK):
                read(dve, ("f1", o), b)
                r = nc.vector.tensor_reduce(out=am[:, o:o + 1], in_=y[:, o, :], axis=AX_X, op=ALU.max,
                                            apply_absolute_value=True)
                r.then_inc(S["clipped"], 1)
            dve.wait_ge(S["clipped"], b * (FK + 2 * KC) + FK)
            scale_of(b, 0, FK)
            for k in range(FK):
                dve.wait_ge(S["g_ready"], b * FK + k + 1)
                if k >= NH:
                    dve.wait_ge(S["h_used"], b * (FK - 1) + k - NH + 1)
                nc.vector.tensor_scalar(h[:, k % NH, 0, :], y[:, k, :], CLIP, None, ALU.min).then_inc(S["hh_ready"], 1)
                dve.wait_ge(S["hh_ready"], b * FK + k + 1)
                nc.vector.scalar_tensor_tensor(out=h[:, k % NH, 1, :], in0=y[:, k, :], scalar=CLIP,
                                               in1=h[:, k % NH, 0, :], op0=ALU.min, op1=ALU.subtract)\
                    .then_inc(S["hl_ready"], 1)
            for m in range(KC):
                read(dve, ("f2", m), b)
                nc.vector.tensor_reduce(out=am[:, m:m + 1], in_=y[:, m, :], axis=AX_X, op=ALU.max,
                                        apply_absolute_value=True).then_inc(S["clipped"], 1)
            dve.wait_ge(S["clipped"], b * (FK + 2 * KC) + FK + KC)
            scale_of(b, 1, KC)
            dve.wait_ge(S["s_ready"], b * 2 + 2)
            for m in range(KC):
                nc.vector.tensor_scalar(y[:, m, :], y[:, m, :], sc[:, 1:2], CLIP, ALU.mult, ALU.min)\
                    .then_inc(S["clipped"], 1)
            for m in range(KC):
                dve.wait_ge(S["clipped"], b * (FK + 2 * KC) + FK + KC + m + 1)
                nc.vector.scalar_tensor_tensor(out=t[:, m, :], in0=y[:, m, :], scalar=-CLIP, in1=t[:, m, :],
                                               op0=ALU.max, op1=ALU.add).then_inc(S["t_ready"], 1)


_INS = ["x", "L0_conv_qkv_w", "L0_conv_qkv_b", "L0_conv_proj_w", "L0_conv_proj_b", "L0_conv_mlp_w1",
        "L0_conv_mlp_b1", "L0_conv_mlp_w2", "L0_conv_mlp_b2", "L0_ffn_W1", "L0_ffn_b1", "L0_ffn_W2", "L0_ffn_b2"]
_OUTS = [((B, C, HT, WD), "float32")]


def kernel(**inputs):
    import numpy as _np
    import concourse.bacc as _bacc
    from concourse import mybir as _mybir
    from concourse.bass_utils import run_bass_kernel_spmd as _run

    nc = _bacc.Bacc("TRN2", target_bir_lowering=False, num_devices=1)
    arrays, args = {}, []
    for name in _INS:
        a = _np.ascontiguousarray(inputs[name])
        arrays[f"in_{name}_dram"] = a
        args.append(nc.dram_tensor(f"in_{name}_dram", a.shape, _mybir.dt.from_np(a.dtype), kind="ExternalInput").ap())
    for i, (shape, dtype) in enumerate(_OUTS):
        dt = _mybir.dt.from_np(_np.dtype(dtype))
        args.append(nc.dram_tensor(f"out_{i}_dram", shape, dt, kind="ExternalOutput").ap())
    metaformer(nc, *args)
    r = _run(nc, [arrays], core_ids=[0])
    got = tuple(r.results[0][f"out_{i}_dram"] for i in range(len(_OUTS)))
    return got[0]
```

```python
from contextlib import ExitStack

import concourse.bass as bass
from concourse import mybir

F32 = mybir.dt.float32
F16 = mybir.dt.float16
BF16 = mybir.dt.bfloat16
I32 = mybir.dt.int32
ALU = mybir.AluOpType
ACT = mybir.ActivationFunctionType
AX_X = mybir.AxisListType.X
ABSMAX = bass.bass_isa.ReduceOp.absmax

P = 128
B, C, HT, WD = 8, 384, 32, 32
N = HT * WD
KC = C // P
HEADS = 8
D = C // HEADS
PAIRS = HEADS // 2
NT = N // P
RT = P // WD
HALF = 512
MLP = max(32, C // 2)
MH = MLP // 2
FF = 4 * C
FK = FF // P
QB, QEPS = 128.0, 1e-5
CLIP = QB - QEPS
GROUPS = 5
FB = (B // GROUPS) * GROUPS
G1, G2 = FF // GROUPS, C // GROUPS
WS = 16.0
SCALE = D ** -0.5 / (WS * WS)
CS = 2048.0
NR, ND, NDP = HT + NT * RT - RT, 2 * HT - 1, 2 * HT
Z = 6
RING = 3
MX_AT = [0, 2, 3, 3, 3, 3, 2, 0]
QK_ORDER = [0, 3, 1, 4, 2, 5]
PREPARE = {(0, 2): ("mean",), (0, 4): ("var",), (0, 6): ("rstd",),
           (1, 2): ("qk", 0), (1, 4): ("qk", 3), (2, 2): ("qk", 1),
           (2, 4): ("qk", 4), (3, 2): ("qk", 2), (3, 4): ("qk", 5)}


def image_steps(prepare):
    out = []
    for p in range(PAIRS):
        maxima = iter([("m", p + 1, hh, i) for hh in range(2) for i in range(NT)] if p + 1 < PAIRS else [])
        for j in range(NT):
            out += [("s", p, hh, j) for hh in range(2)]
            mx = [next(maxima) for _ in range(MX_AT[j])] if p + 1 < PAIRS else []
            last = (p, j - 1) if j else (p - 1, NT - 1)
            pv = [("pv", *last, f) for f in range(2)] if last[0] >= 0 else []
            for n in range(3):
                out += mx[n:n + 1] + pv[n:n + 1]
            if p > 0 and j < 3:
                out += [[("sums", p - 1), ("ot", p - 1), ("rb", p - 1)][j]]
            if p + 1 < PAIRS and j == NT - 2:
                out += [("ct", p + 1)]
            if prepare and (p, j) in PREPARE:
                out += [PREPARE[p, j]]
    q = PAIRS - 1
    mx = FIRST_MAX if prepare else []
    v = [[t] if prepare else [] for t in V_TILES]
    out += mx[0:3] + [("pv", q, NT - 1, f) for f in range(2)] + [("sums", q)] + v[0] + mx[3:6] + [("ot", q)]
    out += v[1] + mx[6:9] + v[2] + mx[9:12] + [("rb", q)] + v[3] + mx[12:16]
    out += [("proj", 0)] + ([("ct", PAIRS)] if prepare else []) + [("proj", m) for m in range(1, KC)]
    return out


FIRST_MAX = [("m", PAIRS, hh, i) for hh in range(2) for i in range(NT)]
LN_TILES = [("mean",), ("var",), ("rstd",)]
QK_TILES = [("qk", t) for t in QK_ORDER]
V_TILES = [("v", t) for t in range(NT // 2)]
PROLOGUE = LN_TILES + QK_TILES + V_TILES + FIRST_MAX + [("ct", PAIRS)]
F1_TILES = [("f1", o) for o in range(FK)]
F2_TILES = [("f2", m) for m in range(KC)]


def image_tiles(prepare):
    return [t for t in image_steps(prepare) if t[0] not in ("pv", "sums")]


class Round:

    def __init__(self, names, before, times=1, own=()):
        self.uses, self.place = [0] * len(before), {}
        k = 0
        for name in names:
            slot = RING if name in own else k % RING
            k += name not in own
            self.place[name] = (slot, before[slot] + self.uses[slot])
            self.uses[slot] += 1
        self.after = [a + times * u for a, u in zip(before, self.uses)]
        self.n = 0

    def at(self, n):
        self.n = n
        return self

    def count(self, tile):
        slot, c = self.place[tile]
        return slot, (c if isinstance(self.n, int) else self.n * self.uses[slot] + c)


def tile_waits(bufs, ready, free):

    def taken(eng, tile, r):
        slot, c = r.count(tile)
        eng.wait_ge(free[slot], c + 1)
        return bufs[slot], ready[slot]

    def filled(eng, tile, r):
        slot, c = r.count(tile)
        eng.wait_ge(ready[slot], c + 1)
        return bufs[slot], free[slot]

    def read(eng, tile, r, into=None):
        slot, c = r.count(tile)
        if into is None or r.place[into][0] != slot:
            eng.wait_ge(free[slot], c + 2)

    return taken, filled, read


def metaformer(nc, x, qkv_w, qkv_b, proj_w, proj_b, mlp_w1, mlp_b1, mlp_w2, mlp_b2, W1, b1, W2, b2, out):
    x_v = x.rearrange("b (k p) h w -> b p k (h w)", p=P)
    out_v = out.rearrange("b (k p) h w -> b p k (h w)", p=P)
    tab = nc.dram_tensor("tab", (HEADS, ND * NDP), F32, kind="Internal").ap()
    tabr = nc.dram_tensor("tabr", (HEADS, ND * NDP), BF16, kind="Internal").ap()
    win = nc.dram_tensor("win", (WD, HEADS, ND, WD), F32, kind="Internal").ap()
    winr = nc.dram_tensor("winr", (WD, HEADS, ND, WD), BF16, kind="Internal").ap()
    qk_d = nc.dram_tensor("qk_d", (B, 2, 2 * C, N), F16, kind="Internal").ap()

    with ExitStack() as top:
        def sbuf(ctx, name, shape, dt=F32):
            return ctx.enter_context(nc.sbuf_tensor(name, shape, dt))

        ident = sbuf(top, "ident", [P, P])
        mean_w = sbuf(top, "mean_w", [P, P])
        ring = [top.enter_context(nc.psum_tensor(f"ring{i}", [P, 2 * HALF], F32)) for i in range(RING)]
        acc = top.enter_context(nc.psum_tensor("acc", [P, 2 * HALF], F32))

        with ExitStack() as att:
            T = {
                "bias": sbuf(att, "bias", [P, HEADS, NR * WD]),
                "wh": sbuf(att, "wh", [P, KC, 3 * C], F16),
                "wl": sbuf(att, "wl", [P, KC, 3 * C], F16),
                "wp": sbuf(att, "wp", [P, PAIRS, C]),
                "qkb": sbuf(att, "qkb", [P, 2 * KC]),
                "pb": sbuf(att, "pb", [P, KC]),
            }
            with ExitStack() as ctx:
                setup_attention(nc, ctx, sbuf, T, ident, mean_w, ring, qkv_w, qkv_b, proj_w, proj_b,
                                mlp_w1, mlp_b1, mlp_w2, mlp_b2, tab, tabr)
            with ExitStack() as ctx:
                attention(nc, ctx, sbuf, T, ident, mean_w, ring, acc, x_v, out_v, tab, tabr, win, winr, qk_d)
        with ExitStack() as ffn:
            T = {
                "w1t": sbuf(ffn, "w1t", [P, KC, FF], F16),
                "w2t": sbuf(ffn, "w2t", [P, FK, C], F16),
                "b1s": sbuf(ffn, "b1s", [P, FK]),
                "b2s": sbuf(ffn, "b2s", [P, KC]),
            }
            with ExitStack() as ctx:
                setup_ffn(nc, ctx, sbuf, T, ident, mean_w, ring, acc, W1, b1, W2, b2)
            with ExitStack() as ctx:
                feed_forward(nc, ctx, sbuf, T, ident, mean_w, ring, acc, out_v)


def setup_attention(nc, ctx, sbuf, T, ident, mean_w, ring, qkv_w, qkv_b, proj_w, proj_b,
                    mlp_w1, mlp_b1, mlp_w2, mlp_b2, tab, tabr):
    def sem(name):
        return ctx.enter_context(nc.semaphore(name))

    NG, PTS = 8, ND * NDP
    CH = PTS // NG
    wtmp = sbuf(ctx, "wtmp", [P, KC, 3 * C])
    bv = sbuf(ctx, "bv", [P, PAIRS])
    pb0 = sbuf(ctx, "pb0", [P, KC])
    w1s = sbuf(ctx, "w1s", [2, MLP])
    b1c = sbuf(ctx, "b1c", [MH, 2])
    w2c = sbuf(ctx, "w2c", [MH, 2, HEADS])
    b2c = sbuf(ctx, "b2c", [HEADS, 1])
    gx = sbuf(ctx, "gx", [1, PTS])
    grid = sbuf(ctx, "grid", [2, PTS])
    hid = sbuf(ctx, "hid", [MH, 2, 2, CH])
    tab_s = sbuf(ctx, "tab_s", [HEADS, PTS])
    tabr_s = sbuf(ctx, "tabr_s", [HEADS, PTS], BF16)
    loads, wload, cst, pads, gridi, grid_in, gridf = (
        sem(n) for n in ("loads", "wload", "cst", "pads", "gridi", "grid_in", "gridf"))
    wh_ready, hidp, hidr, tabp, tabf = (sem(n) for n in ("wh_ready", "hidp", "hidr", "tabp", "tabf"))
    tab_out, pbp, wdone = (sem(n) for n in ("tab_out", "pbp", "wdone"))
    block = ctx.enter_context(nc.Block())

    @block.sync
    def _(sp):
        with nc.allow_non_contiguous_dma(reason="biases by partition"):
            sp.dma_start(w1s[:, :], mlp_w1).then_inc(loads, 16)
            sp.dma_start(b1c[:, :], mlp_b1.rearrange("(a p) -> p a", a=2)).then_inc(loads, 16)
            sp.dma_start(w2c[:, :, :], mlp_w2.rearrange("(a p) n -> p a n", a=2)).then_inc(loads, 16)
            sp.dma_start(b2c[:, :], mlp_b2.rearrange("(p a) -> p a", a=1)).then_inc(loads, 16)
            sp.dma_start(T["qkb"][:, :], qkv_b[0:2 * C].rearrange("(k p) -> p k", p=P)).then_inc(loads, 16)
            sp.dma_start(pb0[:, :], proj_b.rearrange("(k p) -> p k", p=P)).then_inc(loads, 16)
            sp.wait_ge(gridi, 2)
            sp.dma_start(grid[1:2, :], gx[:, :]).then_inc(grid_in, 16)
            sp.dma_start(wtmp[:, :, :], qkv_w.rearrange("(k p) n -> p k n", p=P)).then_inc(wload, 16)
            sp.wait_ge(pads, 2)
            for t in range(2):
                sp.dma_start(T["wp"][64 * t:64 * t + D, :, :],
                             proj_w.rearrange("(p t d) n -> t d p n", t=2, d=D)[t]).then_inc(loads, 16)
                sp.dma_start(bv[64 * t:64 * t + D, :],
                             qkv_b[2 * C:3 * C].rearrange("(p t d) -> t d p", t=2, d=D)[t]).then_inc(loads, 16)
        sp.wait_ge(tabf, 2 * NG)
        sp.dma_start(tab, tab_s[:, :]).then_inc(tab_out, 16)
        sp.dma_start(tabr[:, 0:PTS - 1], tabr_s[:, 1:PTS]).then_inc(tab_out, 16)
        sp.wait_ge(tab_out, 32)

    @block.gpsimd
    def _(pool):
        nc.gpsimd.iota(grid[:, :], [[1, ND], [0, NDP]], base=-(HT - 1), channel_multiplier=0,
                       allow_small_or_imprecise_dtypes=True).then_inc(gridi, 1)
        nc.gpsimd.iota(gx[:, :], [[0, ND], [1, NDP]], base=-(WD - 1), channel_multiplier=0,
                       allow_small_or_imprecise_dtypes=True).then_inc(gridi, 1)
        nc.gpsimd.memset(T["wp"][:, :, :], 0.0).then_inc(pads, 1)
        nc.gpsimd.memset(bv[:, :], 0.0).then_inc(pads, 1)
        nc.gpsimd.memset(mean_w[:, :], 1.0 / C).then_inc(cst, 1)
        nc.gpsimd.memset(ident[:, :], 0.0).then_inc(cst, 1)
        pool.wait_ge(cst, 2)
        nc.gpsimd.affine_select(out=ident[:, :], in_=ident[:, :], compare_op=ALU.not_equal, fill=1.0, base=0,
                                pattern=[[-1, P]], channel_multiplier=1).then_inc(cst, 1)

    @block.scalar
    def _(act):
        act.wait_ge(loads, 16 * 10)
        for c in range(NG):
            act.wait_ge(hidp, c + 1)
            if c >= 2:
                act.wait_ge(tabp, c - 1)
            for a in range(2):
                nc.scalar.activation(hid[:, c % 2, a, :], ring[c % 2][0:MH, a * HALF:a * HALF + CH], ACT.Gelu,
                                     bias=b1c[:, a:a + 1]).then_inc(hidr, 1)
        act.wait_ge(wload, 16)
        for k in range(KC):
            nc.scalar.activation(T["wh"][:, k, :], wtmp[:, k, :], ACT.Copy, scale=WS).then_inc(wh_ready, 1)

    @block.tensor
    def _(pe):
        def first_layer(c):
            if c >= 2:
                pe.wait_ge(hidr, 2 * (c - 1))
            for a in range(2):
                last = nc.tensor.matmul(ring[c % 2][0:MH, a * HALF:a * HALF + CH], w1s[:, a * MH:(a + 1) * MH],
                                        grid[:, c * CH:(c + 1) * CH], start=True, stop=True)
            last.then_inc(hidp, 1)

        pe.wait_ge(loads, 16 * 10)
        pe.wait_ge(gridf, 1)
        first_layer(0)
        for c in range(NG):
            if c + 1 < NG:
                first_layer(c + 1)
            pe.wait_ge(hidr, 2 * (c + 1))
            if c >= 2:
                pe.wait_ge(tabf, 2 * (c - 1))
            at = (c % 2) * HALF
            for a in range(2):
                last = nc.tensor.matmul(ring[2][0:HEADS, at:at + CH], w2c[:, a, :], hid[:, c % 2, a, :],
                                        start=a == 0, stop=a == 1)
            last.then_inc(tabp, 1)
        pe.wait_ge(tabf, 2 * NG)
        for m in range(KC):
            for p in range(PAIRS):
                last = nc.tensor.matmul(ring[2][:, m:m + 1], T["wp"][:, p, m * P:(m + 1) * P], bv[:, p:p + 1],
                                        start=p == 0, stop=p == PAIRS - 1)
        last.then_inc(pbp, 1)

    @block.vector
    def _(dve):
        dve.wait_ge(gridi, 1)
        dve.wait_ge(grid_in, 16)
        nc.vector.tensor_scalar(grid[:, :], grid[:, :], 1.0 / (HT - 1), None, ALU.mult).then_inc(gridf, 1)
        dve.wait_ge(loads, 16 * 10)
        nc.vector.tensor_scalar(T["qkb"][:, :], T["qkb"][:, :], WS, None, ALU.mult).then_inc(wdone, 1)
        for c in range(NG):
            dve.wait_ge(tabp, c + 1)
            half = ring[2][0:HEADS, (c % 2) * HALF:(c % 2) * HALF + CH]
            nc.vector.tensor_scalar(tab_s[:, c * CH:(c + 1) * CH], half, b2c[:, 0:1], None, ALU.add).then_inc(tabf, 1)
            whole = tabr_s[:, :]
            turned = bass.AP(whole.tensor, whole.offset + PTS - 1 - c * CH, [list(whole.ap[0]), [-1, CH]])
            nc.vector.tensor_scalar(turned, half, b2c[:, 0:1], 1.0 / SCALE, ALU.add, ALU.mult).then_inc(tabf, 1)
        for k in range(KC):
            dve.wait_ge(wh_ready, k + 1)
            nc.vector.scalar_tensor_tensor(out=T["wl"][:, k, :], in0=wtmp[:, k, :], scalar=WS, in1=T["wh"][:, k, :],
                                           op0=ALU.mult, op1=ALU.subtract).then_inc(wdone, 1)
        dve.wait_ge(pbp, 1)
        nc.vector.tensor_tensor(T["pb"][:, :], ring[2][:, 0:KC], pb0[:, :], ALU.add).then_inc(wdone, 1)


def attention(nc, ctx, sbuf, T, ident, mean_w, ring, acc, x_v, out_v, tab, tabr, win, winr, qk_d):
    def sem(name):
        return ctx.enter_context(nc.semaphore(name))

    first = Round(PROLOGUE, [0] * RING)
    body = Round(image_tiles(True), first.after, B - 1)
    final = Round(image_tiles(False), body.after)
    bias, wh, wl, wp, qkb, pb = (T[k] for k in ("bias", "wh", "wl", "wp", "qkb", "pb"))
    xc = sbuf(ctx, "xc", [P, KC, N])
    xn = sbuf(ctx, "xn", [P, 2, KC, N], F16)
    sq = xn[:, :, :, :].rearrange("p s k n -> p (s k n)").bitcast(F32).rearrange("p (k n) -> p k n", n=N)
    st = sbuf(ctx, "st", [P, 2, 2, N], F16)
    res2 = sbuf(ctx, "res2", [P, N])
    res = [st[:, i, :, :].rearrange("p s n -> p (s n)").bitcast(F32) for i in range(2)] + [res2[:, :]]
    q2 = sbuf(ctx, "q2", [P, 2, 2, N], F16)
    kh = sbuf(ctx, "kh", [P, 2, 2, N], F16)
    kl = sbuf(ctx, "kl", [P, 2, 2, N], F16)
    ur = sbuf(ctx, "ur", [P, 2, NR * WD], BF16)
    v = sbuf(ctx, "v", [P, NT, HEADS, 64])
    zp = sbuf(ctx, "zp", [P, Z, N])
    xo = sbuf(ctx, "xo", [P, PAIRS, N])
    cm = sbuf(ctx, "cm", [P, 2, 2 * NT])
    ct = sbuf(ctx, "ct", [2 * NT, 2, P], F16)
    rc = sbuf(ctx, "rc", [P, NT, 2])
    std = sbuf(ctx, "std", [P, NT])
    rstd = sbuf(ctx, "rstd", [P, NT])
    eps = sbuf(ctx, "eps", [P, 1])

    ready = [sem(f"ready{i}") for i in range(RING)]
    free = [sem(f"free{i}") for i in range(RING)]
    taken, filled, read = tile_waits(ring, ready, free)
    names = ("consts", "x_in", "xc_ready", "sq_ready", "rstd_ready", "xn_ready", "xh_ready", "xl_ready", "win_out",
             "winr_out", "bias_in", "sh_ready", "res_in", "ur_in", "p_ready", "pv_done", "osb_ready", "stored",
             "step", "image")
    S = {n: sem(n) for n in names}
    st_out = [sem(f"st_out{i}") for i in range(2)]
    qk_in = [sem(f"qk_in{i}") for i in range(2)]
    max_in = [sem(f"max_in{i}") for i in range(2)]
    block = ctx.enter_context(nc.Block())
    QK_IN, NTILE = 16 * 6, PAIRS * NT * 2

    def tab_rows(t, c):
        return t.rearrange("h (a w) -> h a w", w=NDP)[:, :, WD - 1 - c:2 * WD - 1 - c]

    def load_x(sp, im):
        sp.dma_start(xc[:, :, :], x_v[bass.ds(im, 1)].squeeze(0)).then_inc(S["x_in"], 16)

    def store_block(sp, t, im, r):
        read(sp, ("qk", t), r)
        i = QK_ORDER.index(t) % 2
        for s in range(2):
            sp.dma_start(qk_d[bass.ds(im, 1), s, t * P:(t + 1) * P, :].squeeze(0),
                         st[:, i, s, :]).then_inc(st_out[i], 16)

    def load_pair(sp, p, im):
        i, h = p % 2, 2 * p * D
        for s in range(2):
            rows = slice(s * D, (s + 1) * D)
            q = qk_d[bass.ds(im, 1), s, h:h + 2 * D, :].squeeze(0).rearrange("(h d) n -> d h n", d=D)
            sp.dma_start(q2[rows, i, :, :], q).then_inc(qk_in[i], 16)
            for part, dst in ((0, kh), (1, kl)):
                k = qk_d[bass.ds(im, 1), part, C + h:C + h + 2 * D, :].squeeze(0).rearrange("(h d) n -> d h n", d=D)
                sp.dma_start(dst[rows, i, :, :], k).then_inc(qk_in[i], 16)

    def load_window(sp, p):
        for y in range(RT):
            at = (RT - 1 - y) * WD
            sp.dma_start(ur[y * WD:(y + 1) * WD, :, :],
                         winr.rearrange("c h a w -> c h (a w)")[:, 2 * p:2 * p + 2, at:at + NR * WD])\
                .then_inc(S["ur_in"], 16)

    def max_rows(sp, p, r):
        read(sp, ("ct", p), r)
        for hh in range(2):
            sp.dma_start(q2[2 * D:2 * D + 1, p % 2, hh, :],
                         ct[hh * NT:(hh + 1) * NT, p % 2, :]).then_inc(max_in[p % 2], 16)

    @block.sync
    def _(sp):
        def image(b, r, prepare):
            if prepare:
                sp.wait_ge(S["xl_ready"], b * KC + KC)
                sp.sem_inc(S["image"], 1)
                load_x(sp, b + 1)
            for kind, *at in image_steps(prepare):
                if kind == "qk":
                    store_block(sp, *at, b + 1, r)
                elif kind == "ct":
                    max_rows(sp, *at, r)
                    if at[0] + 1 < PAIRS or prepare:
                        load_window(sp, (at[0] + 1) % PAIRS)
                elif kind == "proj":
                    m, = at
                    read(sp, ("proj", m), r)
                    sp.dma_start(out_v[bass.ds(b, 1), :, m, :].squeeze(0), res[m]).then_inc(S["stored"], 16)
                elif kind == "s" and at[1:] == [1, NT - 1]:
                    p = at[0]
                    if p + 2 < PAIRS or prepare:
                        filled(sp, ("s", p, 1, NT - 1), r)
                        sp.sem_inc(S["image"], 1)
                        if p + 2 >= PAIRS:
                            for i in range(2):
                                sp.wait_ge(st_out[i], b * (32 * KC) + 32 * KC + (32 if p + 2 == PAIRS else 32 * KC))
                        load_pair(sp, (p + 2) % PAIRS, b + (p + 2) // PAIRS)
                    if p == PAIRS - 1:
                        sp.wait_ge(S["stored"], b * (16 * KC) + 1)
                        sp.sem_inc(S["image"], 1)
                        for m in range(KC):
                            sp.dma_start(res[m], x_v[bass.ds(b, 1), :, m, :].squeeze(0)).then_inc(S["res_in"], 16)

        sp.sem_inc(S["stored"], 1)
        load_x(sp, 0)
        for c in range(WD):
            sp.dma_start(win[c], tab_rows(tab, c)).then_inc(S["win_out"], 16)
        for _, t in QK_TILES:
            store_block(sp, t, 0, first.at(0))
        for i in range(2):
            sp.wait_ge(st_out[i], 32 * KC)
        load_pair(sp, 0, 0)
        sp.wait_ge(S["winr_out"], 16 * WD)
        load_window(sp, 0)
        load_pair(sp, 1, 0)
        sp.wait_ge(S["win_out"], 16 * WD)
        for y in range(RT):
            at = (RT - 1 - y) * WD
            sp.dma_start(bias[y * WD:(y + 1) * WD, :, :],
                         win.rearrange("c h a w -> c h (a w)")[:, :, at:at + NR * WD]).then_inc(S["bias_in"], 16)
        max_rows(sp, PAIRS, first.at(0))
        load_window(sp, 1)
        with sp.Fori(0, B - 1) as b:
            image(b, body.at(b), True)
        image(B - 1, final.at(0), False)
        sp.wait_ge(S["stored"], 16 * KC * B + 1)

    @block.gpsimd
    def _(pool):
        nc.gpsimd.memset(v[:, :, :, :], 1.0).then_inc(S["consts"], 1)
        pool.wait_ge(S["consts"], 1)
        nc.gpsimd.memset(kh[2 * D:P, :, :, :], CS).then_inc(S["consts"], 1)
        pool.wait_ge(S["consts"], 2)
        nc.gpsimd.memset(eps[:, :], 1e-6).then_inc(S["consts"], 1)
        layernorm_pool(nc, pool, 0, S, xc, xn)
        with pool.Fori(0, B - 1) as b:
            layernorm_pool(nc, pool, b + 1, S, xc, xn)

    @block.tensor
    def _(pe):
        def scores(p, hh, j, r):
            buf, done = taken(pe, ("s", p, hh, j), r)
            i = p % 2
            for f in range(2):
                cols = slice(f * HALF, (f + 1) * HALF)
                nc.tensor.matmul(buf[:, cols], kh[0:2 * D + 1, i, hh, j * P:(j + 1) * P],
                                 q2[0:2 * D + 1, i, hh, cols], start=True, stop=False)
                last = nc.tensor.matmul(buf[:, cols], kl[0:2 * D, i, hh, j * P:(j + 1) * P],
                                        q2[0:2 * D, i, hh, cols], start=False, stop=True)
            last.then_inc(done, 1)

        def max_scores(p, hh, i, r):
            buf, done = taken(pe, ("m", p, hh, i), r)
            for f in range(2):
                cols = slice(f * HALF, (f + 1) * HALF)
                last = nc.tensor.matmul(buf[:, cols], q2[0:2 * D, p % 2, hh, i * P:(i + 1) * P],
                                        kh[0:2 * D, p % 2, hh, cols], start=True, stop=True)
            last.then_inc(done, 1)

        def max_transpose(p, r):
            buf, done = taken(pe, ("ct", p), r)
            read(pe, ("m", p, 1, NT - 1), r, ("ct", p))
            nc.tensor.transpose(buf[0:2 * NT, 0:P], cm[:, p % 2, :], ident[:, :]).then_inc(done, 1)

        def values(p, j, f, b):
            k = 2 * NT * p + 2 * j
            if f == 0:
                pe.wait_ge(S["p_ready"], b * NTILE + k + 2)
                if j == 0 and p >= 1:
                    pe.wait_ge(S["osb_ready"], b * PAIRS + p)
            cols = slice(f * HALF, (f + 1) * HALF)
            for hh in range(2):
                last = nc.tensor.matmul(acc[64 * hh:64 * hh + 64, cols], v[:, j, 2 * p + hh, :],
                                        zp[:, (k + hh) % Z, cols], start=j == 0, stop=j == NT - 1)
            if f == 1:
                last.then_inc(S["pv_done"], 2)

        def sums_transpose(p, b, r):
            buf, done = taken(pe, ("ot", p), r)
            pe.wait_ge(S["osb_ready"], b * PAIRS + p + 1)
            for i in range(NT):
                last = nc.tensor.transpose(buf[:, i * P:(i + 1) * P], xo[:, p, i * P:(i + 1) * P], ident[:, :])
            last.then_inc(done, 1)

        def sums_broadcast(p, r):
            buf, done = taken(pe, ("rb", p), r)
            read(pe, ("ot", p), r, ("rb", p))
            for i in range(NT):
                for hh in range(2):
                    last = nc.tensor.matmul(buf[64 * hh:64 * hh + 64, i * P:(i + 1) * P],
                                            rc[:, i, hh:hh + 1].to_broadcast([P, 64]), ident[:, :],
                                            start=True, stop=True)
            last.then_inc(done, 1)

        terms = [(w, s, k) for w, s in ((wh, 0), (wh, 1), (wl, 0)) for k in range(KC)]

        def project_qk(t, im, r):
            buf, done = taken(pe, ("qk", t), r)
            if t == QK_ORDER[0]:
                pe.wait_ge(S["xl_ready"], im * KC + KC)
            for f in range(2):
                cols = slice(f * HALF, (f + 1) * HALF)
                for n, (w, s, k) in enumerate(terms):
                    last = nc.tensor.matmul(buf[:, cols], w[:, k, t * P:(t + 1) * P], xn[:, s, k, cols],
                                            start=n == 0, stop=n == len(terms) - 1)
            last.then_inc(done, 1)

        def project_v(t, r):
            buf, done = taken(pe, ("v", t), r)
            for f in range(2):
                rows = slice((2 * t + f) * P, (2 * t + f + 1) * P)
                for n, (w, s, k) in enumerate(terms):
                    last = nc.tensor.matmul(buf[:, f * HALF:f * HALF + C], xn[:, s, k, rows], w[:, k, 2 * C:3 * C],
                                            start=n == 0, stop=n == len(terms) - 1)
            last.then_inc(done, 1)

        def project_out(m, r):
            buf, done = taken(pe, ("proj", m), r)
            if m == 0:
                read(pe, ("rb", PAIRS - 1), r, ("proj", 0))
            for f in range(2):
                cols = slice(f * HALF, (f + 1) * HALF)
                for p in range(PAIRS):
                    last = nc.tensor.matmul(buf[:, cols], wp[:, p, m * P:(m + 1) * P], xo[:, p, cols],
                                            start=p == 0, stop=p == PAIRS - 1)
            last.then_inc(done, 1)

        def image(b, r, prepare):
            for kind, *at in image_steps(prepare):
                if kind == "s":
                    p, hh, j = at
                    if (hh, j) == (0, 0):
                        pe.wait_ge(max_in[p % 2], b * 64 + 32 * (p // 2 + 1))
                    scores(p, hh, j, r)
                elif kind == "m":
                    p, hh, i = at
                    if (hh, i) == (0, 0):
                        pe.wait_ge(qk_in[p % 2], b * (2 * QK_IN) + QK_IN * (p // 2 + 1))
                    max_scores(p, hh, i, r)
                elif kind == "ct":
                    max_transpose(*at, r)
                elif kind == "pv":
                    values(*at, b)
                elif kind == "ot":
                    sums_transpose(*at, b, r)
                elif kind == "rb":
                    sums_broadcast(*at, r)
                elif kind == "qk":
                    project_qk(*at, b + 1, r)
                elif kind == "v":
                    project_v(*at, r)
                elif kind == "proj":
                    project_out(*at, r)
                elif (kind,) in LN_TILES:
                    layernorm_pe(nc, pe, kind, taken, b + 1, r, S, xc, sq, mean_w, ident, rstd)

        r = first.at(0)
        pe.wait_ge(S["consts"], 3)
        for kind, in LN_TILES:
            layernorm_pe(nc, pe, kind, taken, 0, r, S, xc, sq, mean_w, ident, rstd)
        for _, t in QK_TILES:
            project_qk(t, 0, r)
        for t in range(NT // 2):
            project_v(t, r)
        pe.wait_ge(qk_in[0], QK_IN)
        for _, *at in FIRST_MAX:
            max_scores(*at, r)
        max_transpose(PAIRS, r)
        read(pe, ("v", NT // 2 - 1), r)
        with pe.Fori(0, B - 1) as b:
            image(b, body.at(b), True)
        image(B - 1, final.at(0), False)

    @block.scalar
    def _(act):
        def exps(p, hh, j, r):
            k = 2 * NT * p + 2 * j + hh
            read(act, ("s", p, hh, j), r)
            nc.scalar.activation(zp[:, k % Z, :], zp[:, k % Z, :], ACT.Exp).then_inc(S["p_ready"], 1)

        def max_evac(p, r):
            buf, done = filled(act, ("ct", p), r)
            nc.scalar.activation(ct[:, p % 2, :], buf[0:2 * NT, 0:P], ACT.Copy, scale=-1.0 / CS).then_inc(done, 1)

        def qk_high(t, im, r):
            buf, _ = filled(act, ("qk", t), r)
            n = QK_ORDER.index(t)
            if n >= 2:
                act.wait_ge(st_out[n % 2], im * (32 * KC) + 32 * (n // 2))
            nc.scalar.activation(st[:, n % 2, 0, :], buf[:, :], ACT.Identity, bias=qkb[:, t:t + 1])\
                .then_inc(S["sh_ready"], 1)

        def v_evac(t, r):
            buf, done = filled(act, ("v", t), r)
            for f in range(2):
                last = nc.scalar.activation(v[:, 2 * t + f, :, 0:D],
                                            buf[:, f * HALF:f * HALF + C].rearrange("p (h d) -> p h d", d=D),
                                            ACT.Copy, scale=1.0 / WS)
            last.then_inc(done, 1)

        def image(b, r, prepare):
            for kind, *at in image_steps(prepare):
                if kind == "s":
                    exps(*at, r)
                elif kind == "sums":
                    p, = at
                    act.wait_ge(S["pv_done"], b * NTILE + 2 * NT * (p + 1))
                    nc.scalar.activation(xo[:, p, :], acc[:, :], ACT.Copy).then_inc(S["osb_ready"], 1)
                elif kind == "ct":
                    max_evac(*at, r)
                elif kind == "qk":
                    if at[0] == QK_ORDER[0]:
                        act.wait_ge(S["stored"], b * (16 * KC) + 1)
                    qk_high(*at, b + 1, r)
                elif kind == "v":
                    v_evac(*at, r)
                elif (kind,) in LN_TILES:
                    layernorm_act(nc, act, kind, filled, read, b + 1, r, S, xc, sq, std, eps, xn)

        for f in free:
            act.sem_inc(f, 1)
        for c in range(WD):
            act.dma_start(winr[c], tab_rows(tabr, c)).then_inc(S["winr_out"], 16)
        act.wait_ge(S["consts"], 3)
        r = first.at(0)
        for kind, in LN_TILES:
            layernorm_act(nc, act, kind, filled, read, 0, r, S, xc, sq, std, eps, xn)
        for _, t in QK_TILES:
            qk_high(t, 0, r)
        for t in range(NT // 2):
            v_evac(t, r)
        max_evac(PAIRS, r)
        with act.Fori(0, B - 1) as b:
            image(b, body.at(b), True)
        image(B - 1, final.at(0), False)

    @block.vector
    def _(dve):
        def softmax_in(p, hh, j, b, r):
            buf, done = filled(dve, ("s", p, hh, j), r)
            k = 2 * NT * p + 2 * j + hh
            if k >= Z:
                dve.wait_ge(S["pv_done"], b * NTILE + k - Z + 1)
            at = (NT - 1 - j) * RT * WD
            nc.vector.scalar_tensor_tensor(out=zp[:, k % Z, :], in0=buf[:, :], scalar=SCALE,
                                           in1=bias[:, 2 * p + hh, at:at + N], op0=ALU.mult, op1=ALU.add)\
                .then_inc(done, 1)

        def row_max(p, hh, i, r):
            buf, done = filled(dve, ("m", p, hh, i), r)
            at = (NT - 1 - i) * RT * WD
            n = hh * NT + i
            dve.sem_inc(S["step"], 1)
            nc.vector.tensor_tensor_reduce(out=buf[:, :], in0=buf[:, :], in1=ur[:, hh, at:at + N],
                                           scale=1.0, scalar=-3.0e38, op0=ALU.add, op1=ALU.max,
                                           accum_out=cm[:, p % 2, n:n + 1]).then_inc(done, 1)

        def qk_low(t, im, r):
            n = QK_ORDER.index(t)
            dve.wait_ge(S["sh_ready"], im * (2 * KC) + n + 1)
            buf, done = filled(dve, ("qk", t), r)
            nc.vector.scalar_tensor_tensor(out=st[:, n % 2, 1, :], in0=buf[:, :], scalar=qkb[:, t:t + 1],
                                           in1=st[:, n % 2, 0, :], op0=ALU.add, op1=ALU.subtract).then_inc(done, 1)

        def sums_inverse(p, r):
            buf, done = filled(dve, ("ot", p), r)
            nc.vector.reciprocal(rc[:, :, :], buf[:, :].rearrange("p (i c) -> p i c", c=P)[:, :, D:D + 65:64])\
                .then_inc(done, 1)

        def normalise(p, r):
            buf, done = filled(dve, ("rb", p), r)
            nc.vector.tensor_tensor(xo[:, p, :], xo[:, p, :], buf[:, :], ALU.mult).then_inc(done, 1)

        def image(b, r, prepare):
            late = []
            for kind, *at in image_steps(prepare):
                if kind == "s":
                    softmax_in(*at, b, r)
                    for t in late:
                        qk_low(t, b + 1, r)
                    late = []
                elif kind == "m":
                    p, hh, i = at
                    if (hh, i) == (0, 0):
                        dve.wait_ge(S["ur_in"], b * (64 * PAIRS) + 64 * (p + 1))
                    row_max(p, hh, i, r)
                elif kind == "ot":
                    sums_inverse(*at, r)
                elif kind == "rb":
                    normalise(*at, r)
                elif kind == "qk":
                    late += at
                elif kind == "proj":
                    m, = at
                    if m == 0:
                        dve.wait_ge(S["res_in"], b * (16 * KC) + 16 * KC)
                    buf, done = filled(dve, ("proj", m), r)
                    nc.vector.scalar_tensor_tensor(out=res[m], in0=buf[:, :], scalar=pb[:, m:m + 1],
                                                   in1=res[m], op0=ALU.add, op1=ALU.add).then_inc(done, 1)
                elif (kind,) in LN_TILES:
                    layernorm_dve(nc, dve, kind, filled, read, b + 1, r, S, xc, std, rstd, xc)

        r = first.at(0)
        for kind, in LN_TILES:
            layernorm_dve(nc, dve, kind, filled, read, 0, r, S, xc, std, rstd, xc)
        for _, t in QK_TILES:
            qk_low(t, 0, r)
        dve.wait_ge(S["ur_in"], 64)
        for _, *at in FIRST_MAX:
            row_max(*at, r)
        dve.wait_ge(S["bias_in"], 16 * RT)
        with dve.Fori(0, B - 1) as b:
            image(b, body.at(b), True)
        image(B - 1, final.at(0), False)


def layernorm_pe(nc, pe, kind, taken, im, r, S, xc, sq, mean_w, ident, rstd, x=None):
    buf, done = taken(pe, (kind,), r)
    if kind == "mean":
        pe.wait_ge(S["x_in"], im * 16 + 16)
        x = xc if x is None else x
        for f in range(2):
            cols = slice(f * HALF, (f + 1) * HALF)
            for k in range(KC):
                last = nc.tensor.matmul(buf[:, cols], mean_w[:, :], x[:, k, cols], start=k == 0, stop=k == KC - 1)
    elif kind == "var":
        pe.wait_ge(S["sq_ready"], im * KC + KC)
        for i in range(NT):
            for k in range(KC):
                last = nc.tensor.matmul(buf[:, i:i + 1], sq[:, k, i * P:(i + 1) * P], mean_w[:, 0:1],
                                        start=k == 0, stop=k == KC - 1)
    else:
        pe.wait_ge(S["rstd_ready"], im + 1)
        for i in range(NT):
            last = nc.tensor.matmul(buf[:, i * P:(i + 1) * P], rstd[:, i:i + 1].to_broadcast([P, P]), ident[:, :],
                                    start=True, stop=True)
    last.then_inc(done, 1)


def layernorm_act(nc, act, kind, filled, read, im, r, S, xc, sq, std, eps, xn):
    if kind == "var":
        buf, done = filled(act, ("var",), r)
        nc.scalar.activation(std[:, :], buf[:, 0:NT], ACT.Sqrt, bias=eps[:, 0:1]).then_inc(done, 1)
        return
    for k in range(KC):
        if k == KC - 1:
            read(act, (kind,), r)
        if kind == "mean":
            if k < KC - 1:
                act.wait_ge(S["xc_ready"], im * (KC - 1) + k + 1)
            nc.scalar.activation(sq[:, k, :], xc[:, k, :], ACT.Square).then_inc(S["sq_ready"], 1)
        else:
            if k < KC - 1:
                act.wait_ge(S["xn_ready"], im * (KC - 1) + k + 1)
            nc.scalar.activation(xn[:, 0, k, :], xc[:, k, :], ACT.Copy).then_inc(S["xh_ready"], 1)


def layernorm_dve(nc, dve, kind, filled, read, im, r, S, x, std, rstd, xc):
    if kind == "var":
        read(dve, ("var",), r)
        nc.vector.reciprocal(rstd[:, :], std[:, :]).then_inc(S["rstd_ready"], 1)
        return
    buf, done = filled(dve, (kind,), r)
    if kind == "mean":
        for k in range(KC):
            nc.vector.tensor_tensor(xc[:, k, :], x[:, k, :], buf[:, :], ALU.subtract)\
                .then_inc(S["xc_ready"] if k < KC - 1 else done, 1)
    else:
        dve.wait_ge(S["sq_ready"], im * KC + KC)
        for k in range(KC):
            nc.vector.tensor_tensor(xc[:, k, :], xc[:, k, :], buf[:, :], ALU.mult)\
                .then_inc(S["xn_ready"] if k < KC - 1 else done, 1)


def layernorm_pool(nc, pool, im, S, xc, xn):
    for k in range(KC):
        pool.wait_ge(S["xh_ready"], im * KC + k + 1)
        nc.gpsimd.tensor_tensor(xn[:, 1, k, :], xc[:, k, :], xn[:, 0, k, :], ALU.subtract).then_inc(S["xl_ready"], 1)


def setup_ffn(nc, ctx, sbuf, T, ident, mean_w, ring, acc, W1, b1, W2, b2):
    def sem(name):
        return ctx.enter_context(nc.semaphore(name))

    mats = ((W1, FK, C, G1, T["w1t"]), (W2, KC, FF, G2, T["w2t"]))
    w = [sbuf(ctx, f"w{i}", [P, m[1], m[2]]) for i, m in enumerate(mats)]
    sg = [sbuf(ctx, f"sg{i}", [P, m[1], m[2]], F16) for i, m in enumerate(mats)]
    mask = [sbuf(ctx, f"mask{i}", [P, m[1], GROUPS]) for i, m in enumerate(mats)]
    prod = [sbuf(ctx, f"prod{i}", [P, m[1], GROUPS]) for i, m in enumerate(mats)]
    rs = [sbuf(ctx, f"rs{i}", [P, m[1]]) for i, m in enumerate(mats)]
    gs = [sbuf(ctx, f"gs{i}", [P, GROUPS]) for i, m in enumerate(mats)]
    gm = [sbuf(ctx, f"gm{i}", [P, GROUPS]) for i, m in enumerate(mats)]
    rm = [sbuf(ctx, f"rm{i}", [P, m[1]]) for i, m in enumerate(mats)]
    live = [sbuf(ctx, f"live{i}", [P, m[1]]) for i, m in enumerate(mats)]
    idh = sbuf(ctx, "idh", [P, P], F16)
    w_in, b_in, masks, sums, group, chain, signs, tp, tc = (
        sem(n) for n in ("w_in", "b_in", "masks", "sums", "group", "chain", "signs", "tp", "tc"))
    block = ctx.enter_context(nc.Block())
    blocks = [(i, r, c) for i, m in enumerate(mats) for r in range(m[1]) for c in range(m[2] // P)]
    lots = [blocks[n:n + 4] for n in range(0, len(blocks), 4)]

    @block.sync
    def _(sp):
        for i, m in enumerate(mats):
            sp.dma_start(w[i][:, :, :], m[0].rearrange("(k p) n -> p k n", p=P)).then_inc(w_in, 16)
        with nc.allow_non_contiguous_dma(reason="biases by partition"):
            sp.dma_start(T["b1s"][:, :], b1.rearrange("(k p) -> p k", p=P)).then_inc(b_in, 16)
            sp.dma_start(T["b2s"][:, :], b2.rearrange("(k p) -> p k", p=P)).then_inc(b_in, 16)
        sp.wait_ge(b_in, 32)

    @block.gpsimd
    def _(pool):
        n = 0
        for i, m in enumerate(mats):
            nc.gpsimd.memset(mask[i][:, :, :], 1.0).then_inc(masks, 1)
            for base, mult in ((0, 1), (m[3] - 1, -1)):
                n += 1
                pool.wait_ge(masks, n)
                nc.gpsimd.affine_select(out=mask[i][:, :, :], in_=mask[i][:, :, :], compare_op=ALU.is_ge, fill=0.0,
                                        base=base, pattern=[[mult * P, m[1]], [-mult * m[3], GROUPS]],
                                        channel_multiplier=mult).then_inc(masks, 1)
            n += 1

    @block.scalar
    def _(act):
        nc.scalar.activation(idh[:, :], ident[:, :], ACT.Copy).then_inc(signs, 1)
        for i, m in enumerate(mats):
            act.wait_ge(chain, 6 * (i + 1))
            for r in range(m[1]):
                nc.scalar.activation(sg[i][:, r, :], w[i][:, r, :], ACT.Sign, bias=rm[i][:, r:r + 1]).then_inc(signs, 1)

    @block.vector
    def _(dve):
        dve.wait_ge(w_in, 32)
        dve.wait_ge(masks, 6)
        n = 0

        def link(ins):
            nonlocal n
            n += 1
            ins.then_inc(chain, 1)
            dve.wait_ge(chain, n)

        for i, m in enumerate(mats):
            link(nc.vector.tensor_reduce(out=rs[i][:, :], in_=w[i][:, :, :], axis=AX_X, op=ALU.add))
            link(nc.vector.tensor_tensor(prod[i][:, :, :], mask[i][:, :, :],
                                         rs[i][:, :].unsqueeze(2).to_broadcast([P, m[1], GROUPS]), ALU.mult))
            nc.vector.tensor_reduce(out=gs[i][:, :], in_=prod[i][:, :, :].rearrange("p k g -> p g k"), axis=AX_X,
                                    op=ALU.add).then_inc(sums, 1)
            dve.wait_ge(group, i + 1)
            link(nc.vector.tensor_scalar(gm[i][:, :], acc[:, HALF * i:HALF * i + GROUPS], -float(C) / (m[3] * m[2]),
                                         None, ALU.mult))
            link(nc.vector.tensor_tensor(prod[i][:, :, :], mask[i][:, :, :],
                                         gm[i][:, :].unsqueeze(1).to_broadcast([P, m[1], GROUPS]), ALU.mult))
            link(nc.vector.tensor_reduce(out=live[i][:, :], in_=mask[i][:, :, :], axis=AX_X, op=ALU.add))
            link(nc.vector.tensor_reduce(out=rm[i][:, :], in_=prod[i][:, :, :], axis=AX_X, op=ALU.add))
        done = 1
        for i, m in enumerate(mats):
            r = m[1] - 1
            done += m[1]
            dve.wait_ge(signs, done)
            nc.vector.tensor_scalar(sg[i][:, r, :], sg[i][:, r, :], live[i][:, r:r + 1], None, ALU.mult)\
                .then_inc(chain, 1)
        for q, lot in enumerate(lots):
            dve.wait_ge(tp, q + 1)
            for n, (i, r, c) in enumerate(lot):
                src = ring[q % RING][:, 0:HALF].bitcast(F16)[:, n * P:(n + 1) * P]
                last = nc.vector.tensor_copy(mats[i][4][:, c, r * P:(r + 1) * P], src)
            last.then_inc(tc, 1)

    @block.tensor
    def _(pe):
        for i in range(2):
            pe.wait_ge(sums, i + 1)
            nc.tensor.matmul(acc[:, HALF * i:HALF * i + GROUPS], mean_w[:, :], gs[i][:, :], start=True, stop=True)\
                .then_inc(group, 1)
        pe.wait_ge(signs, 1 + FK + KC)
        pe.wait_ge(chain, 14)
        for q, lot in enumerate(lots):
            if q >= RING:
                pe.wait_ge(tc, q - RING + 1)
            for n, (i, r, c) in enumerate(lot):
                last = nc.tensor.transpose(ring[q % RING][:, 0:HALF].bitcast(F16)[:, n * P:(n + 1) * P],
                                           sg[i][:, r, c * P:(c + 1) * P], idh[:, :])
            last.then_inc(tp, 1)


def feed_forward(nc, ctx, sbuf, T, ident, mean_w, ring, acc, out_v):
    def sem(name):
        return ctx.enter_context(nc.semaphore(name))

    own = set(LN_TILES)
    first = Round(LN_TILES + F1_TILES, [0] * (RING + 1), 1, own)
    body = Round(F2_TILES + LN_TILES + F1_TILES, first.after, FB - 1, own)
    final = Round(F2_TILES, body.after, 1, own)
    w1t, w2t, b1s, b2s = (T[k] for k in ("w1t", "w2t", "b1s", "b2s"))
    NH = 4
    LN_AT = {0: "mean", 3: "var", 5: "rstd"}
    t = sbuf(ctx, "t", [P, 2, KC, N])
    xc = sbuf(ctx, "fxc", [P, KC, N])
    sq = sbuf(ctx, "fsq", [P, KC, N])
    xn = sbuf(ctx, "fxn", [P, 2, KC, N], F16)
    y = sbuf(ctx, "y", [P, FK, N])
    y2 = sbuf(ctx, "y2", [P, KC, N])
    h = sbuf(ctx, "h", [P, NH, 2, N], F16)
    am = sbuf(ctx, "am", [P, 2, FK])
    am1 = sbuf(ctx, "am1", [P, 2])
    gam = sbuf(ctx, "gam", [P, 2])
    ge = sbuf(ctx, "ge", [P, 2])
    gr = sbuf(ctx, "gr", [P, 2])
    sc = sbuf(ctx, "sc", [P, 2])
    std = sbuf(ctx, "fstd", [P, NT])
    rstd = sbuf(ctx, "frstd", [P, NT])
    eps = sbuf(ctx, "feps", [P, 1])
    ready = [sem(f"fready{i}") for i in range(RING + 1)]
    free = [sem(f"ffree{i}") for i in range(RING + 1)]
    taken, filled, read = tile_waits([*ring, acc], ready, free)
    names = ("consts", "x_in", "xc_ready", "sq_ready", "rstd_ready", "xn_ready", "xh_ready", "xl_ready",
             "am_ready0", "am_ready1", "gam_ready0", "gam_ready1", "chain0", "chain1", "s_ready0", "s_ready1",
             "max0", "max1", "g_ready", "hh_ready", "hl_ready", "h_used", "clipped", "t_ready", "stored", "step",
             "image")
    S = {n: sem("f_" + n) for n in names}
    block = ctx.enter_context(nc.Block())
    assert FB % 2 == 1 and FB > 2

    def in_pairs(eng, image, last):
        with eng.Fori(0, FB - 1, 2) as b:
            for i in range(2):
                image(b + i, i, body.at(b + i), True)
        last(image)

    def final_image(image):
        image(FB - 1, (FB - 1) % 2, final.at(0), False)

    @block.sync
    def _(sp):
        def load(im, i):
            sp.dma_start(t[:, i, :, :], out_v[bass.ds(im, 1)].squeeze(0)).then_inc(S["x_in"], 16)

        def image(b, i, r, more):
            if more:
                sp.wait_ge(S["x_in"], b * 16 + 16)
                load(b + 1, 1 - i)
            sp.wait_ge(S["t_ready"], b * KC + KC)
            sp.dma_start(out_v[bass.ds(b, 1)].squeeze(0), t[:, i, :, :]).then_inc(S["stored"], 16)
            sp.wait_ge(S["stored"], b * 16 + 16)
            sp.sem_inc(S["image"], 1)

        load(0, 0)
        in_pairs(sp, image, final_image)
        sp.wait_ge(S["stored"], 16 * FB)

    @block.gpsimd
    def _(pool):
        def all_max(b, s):
            pool.wait_ge(S[f"am_ready{s}"], b + 1)
            pool.sem_inc(S["step"], 1)
            nc.gpsimd.partition_all_reduce(gam[:, s:s + 1], am1[:, s:s + 1], P, ABSMAX)\
                .then_inc(S[f"gam_ready{s}"], 1)

        nc.gpsimd.memset(eps[:, :], 1e-5).then_inc(S["consts"], 1)
        layernorm_pool(nc, pool, 0, S, xc, xn)
        with pool.Fori(0, FB - 1) as b:
            all_max(b, 0)
            layernorm_pool(nc, pool, b + 1, S, xc, xn)
            all_max(b, 1)
        all_max(FB - 1, 0)
        all_max(FB - 1, 1)

    @block.tensor
    def _(pe):
        def first_layer(im, r):
            for o in range(FK):
                buf, done = taken(pe, ("f1", o), r)
                if o == 0:
                    pe.wait_ge(S["xl_ready"], im * KC + KC)
                for f in range(2):
                    cols = slice(f * HALF, (f + 1) * HALF)
                    for s in range(2):
                        for k in range(KC):
                            last = nc.tensor.matmul(buf[:, cols], w1t[:, k, o * P:(o + 1) * P], xn[:, s, k, cols],
                                                    start=s == 0 and k == 0, stop=s == 1 and k == KC - 1)
                last.then_inc(done, 1)

        def image(b, i, r, more):
            for k in range(FK):
                if more and k in LN_AT:
                    layernorm_pe(nc, pe, LN_AT[k], taken, b + 1, r, S, xc, sq, mean_w, ident, rstd, t[:, 1 - i, :, :])
                if k == 0:
                    accs = [taken(pe, ("f2", m), r) for m in range(KC)]
                pe.wait_ge(S["hl_ready"], b * FK + k + 1)
                for m in range(KC):
                    for f in range(2):
                        cols = slice(f * HALF, (f + 1) * HALF)
                        for s in range(2):
                            last = nc.tensor.matmul(accs[m][0][:, cols], w2t[:, k, m * P:(m + 1) * P],
                                                    h[:, k % NH, s, cols], start=k == 0 and s == 0,
                                                    stop=k == FK - 1 and s == 1)
                    if k == FK - 1:
                        last.then_inc(accs[m][1], 1)
                if k < FK - 1:
                    last.then_inc(S["h_used"], 1)
            if more:
                first_layer(b + 1, r)

        pe.wait_ge(S["consts"], 1)
        r = first.at(0)
        for kind, in LN_TILES:
            layernorm_pe(nc, pe, kind, taken, 0, r, S, xc, sq, mean_w, ident, rstd, t[:, 0, :, :])
        first_layer(0, r)
        in_pairs(pe, image, final_image)

    @block.scalar
    def _(act):
        def first_layer(r):
            for o in range(FK):
                buf, done = filled(act, ("f1", o), r)
                nc.scalar.activation(y[:, o, :], buf[:, :], ACT.Identity, bias=b1s[:, o:o + 1]).then_inc(done, 1)

        def image(b, i, r, more):
            act.wait_ge(S["s_ready0"], b + 1)
            for k in range(FK):
                nc.scalar.activation(y[:, k, :], y[:, k, :], ACT.Gelu, scale=sc[:, 0:1]).then_inc(S["g_ready"], 1)
                if more and k in LN_AT:
                    layernorm_act(nc, act, LN_AT[k], filled, read, b + 1, r, S, xc, sq, std, eps, xn)
            for m in range(KC):
                buf, done = filled(act, ("f2", m), r)
                nc.scalar.activation(y2[:, m, :], buf[:, :], ACT.Identity, bias=b2s[:, m:m + 1]).then_inc(done, 1)
            if more:
                first_layer(r)

        for f in free:
            act.sem_inc(f, 1)
        act.wait_ge(S["consts"], 1)
        r = first.at(0)
        for kind, in LN_TILES:
            layernorm_act(nc, act, kind, filled, read, 0, r, S, xc, sq, std, eps, xn)
        first_layer(r)
        in_pairs(act, image, final_image)

    @block.vector
    def _(dve):
        def largest(src, s, o):
            nc.vector.tensor_reduce(out=am[:, s, o:o + 1], in_=src, axis=AX_X, op=ALU.max,
                                    apply_absolute_value=True).then_inc(S[f"max{s}"], 1)

        def scale_of(b, s, n):
            dve.wait_ge(S[f"max{s}"], b * n + n)
            nc.vector.tensor_reduce(out=am1[:, s:s + 1], in_=am[:, s, 0:n], axis=AX_X, op=ALU.max)\
                .then_inc(S[f"am_ready{s}"], 1)
            dve.wait_ge(S[f"gam_ready{s}"], b + 1)
            nc.vector.tensor_scalar(ge[:, s:s + 1], gam[:, s:s + 1], QEPS, None, ALU.add).then_inc(S[f"chain{s}"], 1)
            dve.wait_ge(S[f"chain{s}"], b * 2 + 1)
            nc.vector.reciprocal(gr[:, s:s + 1], ge[:, s:s + 1]).then_inc(S[f"chain{s}"], 1)
            dve.wait_ge(S[f"chain{s}"], b * 2 + 2)
            nc.vector.tensor_scalar(sc[:, s:s + 1], gr[:, s:s + 1], QB, None, ALU.mult).then_inc(S[f"s_ready{s}"], 1)

        def first_layer(r, os):
            for o in os:
                read(dve, ("f1", o), r)
                largest(y[:, o, :], 0, o)

        def hidden(b, k):
            dve.wait_ge(S["g_ready"], b * FK + k + 1)
            if k >= NH:
                dve.wait_ge(S["h_used"], b * (FK - 1) + k - NH + 1)
            nc.vector.tensor_scalar(h[:, k % NH, 0, :], y[:, k, :], CLIP, None, ALU.min).then_inc(S["hh_ready"], 1)
            dve.wait_ge(S["hh_ready"], b * FK + k + 1)
            nc.vector.scalar_tensor_tensor(out=h[:, k % NH, 1, :], in0=y[:, k, :], scalar=CLIP,
                                           in1=h[:, k % NH, 0, :], op0=ALU.min, op1=ALU.subtract)\
                .then_inc(S["hl_ready"], 1)

        def image(b, i, r, more):
            for k in range(FK):
                hidden(b, k)
                if more and k in LN_AT:
                    layernorm_dve(nc, dve, LN_AT[k], filled, read, b + 1, r, S, t[:, 1 - i, :, :], std, rstd, xc)
            for m in range(KC):
                read(dve, ("f2", m), r)
                largest(y2[:, m, :], 1, m)
            scale_of(b, 1, KC)
            dve.wait_ge(S["s_ready1"], b + 1)
            for m in range(KC):
                nc.vector.tensor_scalar(y2[:, m, :], y2[:, m, :], sc[:, 1:2], CLIP, ALU.mult, ALU.min)\
                    .then_inc(S["clipped"], 1)
            for m in range(KC):
                dve.wait_ge(S["clipped"], b * KC + m + 1)
                nc.vector.scalar_tensor_tensor(out=t[:, i, m, :], in0=y2[:, m, :], scalar=-CLIP, in1=t[:, i, m, :],
                                               op0=ALU.max, op1=ALU.add).then_inc(S["t_ready"], 1)
            if more:
                first_layer(r, range(FK))
                scale_of(b + 1, 0, FK)

        r = first.at(0)
        for kind, in LN_TILES:
            layernorm_dve(nc, dve, kind, filled, read, 0, r, S, t[:, 0, :, :], std, rstd, xc)
        first_layer(r, range(FK))
        scale_of(0, 0, FK)
        in_pairs(dve, image, final_image)


_INS = ["x", "L0_conv_qkv_w", "L0_conv_qkv_b", "L0_conv_proj_w", "L0_conv_proj_b", "L0_conv_mlp_w1",
        "L0_conv_mlp_b1", "L0_conv_mlp_w2", "L0_conv_mlp_b2", "L0_ffn_W1", "L0_ffn_b1", "L0_ffn_W2", "L0_ffn_b2"]
_OUTS = [((B, C, HT, WD), "float32")]


def kernel(**inputs):
    import numpy as _np
    import concourse.bacc as _bacc
    from concourse import mybir as _mybir
    from concourse.bass_utils import run_bass_kernel_spmd as _run

    nc = _bacc.Bacc("TRN2", target_bir_lowering=False, num_devices=1)
    arrays, args = {}, []
    for name in _INS:
        a = _np.ascontiguousarray(inputs[name])
        arrays[f"in_{name}_dram"] = a
        args.append(nc.dram_tensor(f"in_{name}_dram", a.shape, _mybir.dt.from_np(a.dtype), kind="ExternalInput").ap())
    for i, (shape, dtype) in enumerate(_OUTS):
        dt = _mybir.dt.from_np(_np.dtype(dtype))
        args.append(nc.dram_tensor(f"out_{i}_dram", shape, dt, kind="ExternalOutput").ap())
    metaformer(nc, *args)
    r = _run(nc, [arrays], core_ids=[0])
    got = tuple(r.results[0][f"out_{i}_dram"] for i in range(len(_OUTS)))
    return got[0]
```

```python
from contextlib import ExitStack

import concourse.bass as bass
from concourse import mybir

F32 = mybir.dt.float32
F16 = mybir.dt.float16
BF16 = mybir.dt.bfloat16
I32 = mybir.dt.int32
ALU = mybir.AluOpType
ACT = mybir.ActivationFunctionType
AX_X = mybir.AxisListType.X
ABSMAX = bass.bass_isa.ReduceOp.absmax

P = 128
B, C, HT, WD = 8, 384, 32, 32
N = HT * WD
KC = C // P
HEADS = 8
D = C // HEADS
PAIRS = HEADS // 2
NT = N // P
RT = P // WD
HALF = 512
MLP = max(32, C // 2)
MH = MLP // 2
FF = 4 * C
FK = FF // P
QB, QEPS = 128.0, 1e-5
CLIP = QB - QEPS
GROUPS = 5
FB = (B // GROUPS) * GROUPS
G1, G2 = FF // GROUPS, C // GROUPS
WS = 16.0
SCALE = D ** -0.5 / (WS * WS)
CS = 2048.0
NR, ND, NDP = HT + NT * RT - RT, 2 * HT - 1, 2 * HT
Z = 6
RING = 3
MX_AT = [0, 3, 3, 3, 3, 3, 1, 0]
QK_ORDER = [0, 3, 1, 4, 2, 5]
PREPARE = {(0, 2): ("mean",), (0, 4): ("var",), (0, 6): ("rstd",),
           (1, 3): ("qk", 0), (1, 5): ("qk", 3), (2, 3): ("qk", 1),
           (2, 5): ("qk", 4), (3, 2): ("qk", 2), (3, 4): ("qk", 5)}


def image_steps(prepare):
    out = []
    for p in range(PAIRS):
        maxima = iter([("m", p + 1, hh, i) for hh in range(2) for i in range(NT)] if p + 1 < PAIRS else [])
        for j in range(NT):
            out += [("s", p, hh, j) for hh in range(2)]
            mx = [next(maxima) for _ in range(MX_AT[j])] if p + 1 < PAIRS else []
            last = (p, j - 1) if j else (p - 1, NT - 1)
            pv = [("pv", *last, f) for f in range(2)] if last[0] >= 0 else []
            for n in range(3):
                out += pv[n:n + 1] + mx[n:n + 1]
            if p > 0 and j < 3:
                out += [[("sums", p - 1), ("ot", p - 1), ("rb", p - 1)][j]]
            if p + 1 < PAIRS and j == NT - 2:
                out += [("ct", p + 1)]
            if (p, j) in PREPARE and (prepare or PREPARE[p, j] in LN_TILES):
                out += [PREPARE[p, j]]
    q = PAIRS - 1
    mx = FIRST_MAX if prepare else []
    v = [[t] if prepare else [] for t in V_TILES]
    out += mx[0:3] + [("pv", q, NT - 1, f) for f in range(2)] + [("sums", q)] + v[0] + mx[3:6] + [("ot", q)]
    out += v[1] + mx[6:9] + v[2] + mx[9:12] + [("rb", q)] + v[3] + mx[12:16]
    out += [("proj", 0)] + ([("ct", PAIRS)] if prepare else []) + [("proj", m) for m in range(1, KC)]
    return out


FIRST_MAX = [("m", PAIRS, hh, i) for hh in range(2) for i in range(NT)]
LN_TILES = [("mean",), ("var",), ("rstd",)]
QK_TILES = [("qk", t) for t in QK_ORDER]
V_TILES = [("v", t) for t in range(NT // 2)]
PROLOGUE = (QK_TILES[0:4] + FIRST_MAX[0:3] + QK_TILES[4:5] + FIRST_MAX[3:6] + QK_TILES[5:6] + FIRST_MAX[6:10]
            + V_TILES[0:1] + FIRST_MAX[10:13] + V_TILES[1:2] + FIRST_MAX[13:16] + V_TILES[2:3] + [("ct", PAIRS)]
            + V_TILES[3:4])
F1_TILES = [("f1", o) for o in range(FK)]
F2_TILES = [("f2", m) for m in range(KC)]


def image_tiles(prepare):
    return [t for t in image_steps(prepare) if t[0] not in ("pv", "sums")]


class Round:

    def __init__(self, names, before, times=1, own=()):
        self.uses, self.place = [0] * len(before), {}
        k = 0
        for name in names:
            slot = RING if name in own else k % RING
            k += name not in own
            self.place[name] = (slot, before[slot] + self.uses[slot])
            self.uses[slot] += 1
        self.after = [a + times * u for a, u in zip(before, self.uses)]
        self.n = 0

    def at(self, n):
        self.n = n
        return self

    def count(self, tile):
        slot, c = self.place[tile]
        return slot, (c if isinstance(self.n, int) else self.n * self.uses[slot] + c)


def tile_waits(bufs, ready, free):

    def taken(eng, tile, r):
        slot, c = r.count(tile)
        eng.wait_ge(free[slot], c + 1)
        return bufs[slot], ready[slot]

    def filled(eng, tile, r):
        slot, c = r.count(tile)
        eng.wait_ge(ready[slot], c + 1)
        return bufs[slot], free[slot]

    def read(eng, tile, r, into=None):
        slot, c = r.count(tile)
        if into is None or r.place[into][0] != slot:
            eng.wait_ge(free[slot], c + 2)

    return taken, filled, read


def metaformer(nc, x, qkv_w, qkv_b, proj_w, proj_b, mlp_w1, mlp_b1, mlp_w2, mlp_b2, W1, b1, W2, b2, out):
    x_v = x.rearrange("b (k p) h w -> b p k (h w)", p=P)
    out_v = out.rearrange("b (k p) h w -> b p k (h w)", p=P)
    tab = nc.dram_tensor("tab", (HEADS, ND * NDP), F32, kind="Internal").ap()
    tabr = nc.dram_tensor("tabr", (HEADS, ND * NDP), BF16, kind="Internal").ap()
    win = nc.dram_tensor("win", (WD, HEADS, ND, WD), F32, kind="Internal").ap()
    winr = nc.dram_tensor("winr", (WD, HEADS, ND, WD), BF16, kind="Internal").ap()
    qk_d = nc.dram_tensor("qk_d", (B, 2, 2 * C, N), F16, kind="Internal").ap()

    with ExitStack() as top:
        def sbuf(ctx, name, shape, dt=F32):
            return ctx.enter_context(nc.sbuf_tensor(name, shape, dt))

        ident = sbuf(top, "ident", [P, P])
        mean_w = sbuf(top, "mean_w", [P, P])
        xn = sbuf(top, "xn", [P, 2, KC, N], F16)
        L = {
            "xc": sbuf(top, "xc", [P, KC, N]),
            "xn": xn,
            "sq": xn[:, :, :, :].rearrange("p s k n -> p (s k n)").bitcast(F32).rearrange("p (k n) -> p k n", n=N),
            "std": sbuf(top, "std", [P, NT]),
            "rstd": sbuf(top, "rstd", [P, NT]),
            "eps": sbuf(top, "eps", [P, 2]),
        }
        ring = [top.enter_context(nc.psum_tensor(f"ring{i}", [P, 2 * HALF], F32)) for i in range(RING)]
        acc = top.enter_context(nc.psum_tensor("acc", [P, 2 * HALF], F32))

        with ExitStack() as att:
            T = {
                "bias": sbuf(att, "bias", [P, HEADS, NR * WD]),
                "wh": sbuf(att, "wh", [P, KC, 3 * C], F16),
                "wl": sbuf(att, "wl", [P, KC, 3 * C], F16),
                "wp": sbuf(att, "wp", [P, PAIRS, C]),
                "qkb": sbuf(att, "qkb", [P, 2 * KC]),
                "pb": sbuf(att, "pb", [P, KC]),
            }
            with ExitStack() as ctx:
                setup_attention(nc, ctx, sbuf, T, L, ident, mean_w, ring, acc, x_v, qkv_w, qkv_b, proj_w, proj_b,
                                mlp_w1, mlp_b1, mlp_w2, mlp_b2, tab, tabr)
            with ExitStack() as ctx:
                attention(nc, ctx, sbuf, T, L, ident, mean_w, ring, acc, x_v, out_v, tab, tabr, win, winr, qk_d)
        with ExitStack() as ffn:
            T = {
                "w1t": sbuf(ffn, "w1t", [P, KC, FF], F16),
                "w2t": sbuf(ffn, "w2t", [P, FK, C], F16),
                "b1s": sbuf(ffn, "b1s", [P, FK]),
                "b2s": sbuf(ffn, "b2s", [P, KC]),
            }
            with ExitStack() as ctx:
                feed_forward(nc, ctx, sbuf, T, L, ident, mean_w, ring, acc, W1, b1, W2, b2, out_v)


def setup_attention(nc, ctx, sbuf, T, L, ident, mean_w, ring, acc, x_v, qkv_w, qkv_b, proj_w, proj_b,
                    mlp_w1, mlp_b1, mlp_w2, mlp_b2, tab, tabr):
    def sem(name):
        return ctx.enter_context(nc.semaphore(name))

    NG, PTS = 8, ND * NDP
    CH = PTS // NG
    wtmp = sbuf(ctx, "wtmp", [P, KC, 3 * C])
    bv = sbuf(ctx, "bv", [P, PAIRS])
    pb0 = sbuf(ctx, "pb0", [P, KC])
    w1s = sbuf(ctx, "w1s", [2, MLP])
    b1c = sbuf(ctx, "b1c", [MH, 2])
    w2c = sbuf(ctx, "w2c", [MH, 2, HEADS])
    b2c = sbuf(ctx, "b2c", [HEADS, 1])
    gx = sbuf(ctx, "gx", [1, PTS])
    grid = sbuf(ctx, "grid", [2, PTS])
    hid = sbuf(ctx, "hid", [MH, 2, 2, CH])
    tab_s = sbuf(ctx, "tab_s", [HEADS, PTS])
    tabr_s = sbuf(ctx, "tabr_s", [HEADS, PTS], BF16)
    loads, wp_in, wload, cst, pads, gridi, grid_in, gridf = (
        sem(n) for n in ("loads", "wp_in", "wload", "cst", "pads", "gridi", "grid_in", "gridf"))
    wh_ready, hidp, hidr, tabp, tabf = (sem(n) for n in ("wh_ready", "hidp", "hidr", "tabp", "tabf"))
    tab_out, pbp, wdone = (sem(n) for n in ("tab_out", "pbp", "wdone"))
    xc, xn, sq, std, rstd, eps = (L[k] for k in ("xc", "xn", "sq", "std", "rstd", "eps"))
    S = {n: sem("s_" + n) for n in ("x_in", "xc_ready", "sq_ready", "summed", "rstd_ready", "xn_ready", "xh_ready",
                                    "xl_ready")}
    ready, free = ([None] * RING + [sem(f"s_{n}")] for n in ("ready", "free"))
    taken, filled, read = tile_waits([*ring, acc], ready, free)
    r = Round(LN_TILES, [0] * (RING + 1), 1, set(LN_TILES))
    LN_PE = {0: "mean", 3: "var", 4: "rstd"}
    LN_DVE = {0: "mean", 4: "var", 5: "rstd"}
    LN_ACT = {1: "mean", 4: "var", 6: "rstd"}
    W_AT = 2
    block = ctx.enter_context(nc.Block())

    @block.sync
    def _(sp):
        with nc.allow_non_contiguous_dma(reason="biases by partition"):
            sp.dma_start(w1s[:, :], mlp_w1).then_inc(loads, 16)
            sp.dma_start(b1c[:, :], mlp_b1.rearrange("(a p) -> p a", a=2)).then_inc(loads, 16)
            sp.dma_start(w2c[:, :, :], mlp_w2.rearrange("(a p) n -> p a n", a=2)).then_inc(loads, 16)
            sp.dma_start(b2c[:, :], mlp_b2.rearrange("(p a) -> p a", a=1)).then_inc(loads, 16)
            sp.dma_start(T["qkb"][:, :], qkv_b[0:2 * C].rearrange("(k p) -> p k", p=P)).then_inc(loads, 16)
            sp.dma_start(pb0[:, :], proj_b.rearrange("(k p) -> p k", p=P)).then_inc(loads, 16)
            sp.wait_ge(gridi, 2)
            sp.dma_start(grid[1:2, :], gx[:, :]).then_inc(grid_in, 16)
            sp.dma_start(xc[:, :, :], x_v[0]).then_inc(S["x_in"], 16)
            sp.dma_start(wtmp[:, :, :], qkv_w.rearrange("(k p) n -> p k n", p=P)).then_inc(wload, 16)
            sp.wait_ge(pads, 2)
            for t in range(2):
                sp.dma_start(T["wp"][64 * t:64 * t + D, :, :],
                             proj_w.rearrange("(p t d) n -> t d p n", t=2, d=D)[t]).then_inc(wp_in, 16)
                sp.dma_start(bv[64 * t:64 * t + D, :],
                             qkv_b[2 * C:3 * C].rearrange("(p t d) -> t d p", t=2, d=D)[t]).then_inc(wp_in, 16)
        sp.wait_ge(tabf, 2 * NG)
        sp.dma_start(tab, tab_s[:, :]).then_inc(tab_out, 16)
        sp.dma_start(tabr[:, 0:PTS - 1], tabr_s[:, 1:PTS]).then_inc(tab_out, 16)
        sp.wait_ge(tab_out, 32)

    @block.gpsimd
    def _(pool):
        nc.gpsimd.iota(grid[:, :], [[1, ND], [0, NDP]], base=-(HT - 1), channel_multiplier=0,
                       allow_small_or_imprecise_dtypes=True).then_inc(gridi, 1)
        nc.gpsimd.iota(gx[:, :], [[0, ND], [1, NDP]], base=-(WD - 1), channel_multiplier=0,
                       allow_small_or_imprecise_dtypes=True).then_inc(gridi, 1)
        nc.gpsimd.memset(T["wp"][:, :, :], 0.0).then_inc(pads, 1)
        nc.gpsimd.memset(bv[:, :], 0.0).then_inc(pads, 1)
        nc.gpsimd.memset(mean_w[:, :], 1.0 / C).then_inc(cst, 1)
        nc.gpsimd.memset(ident[:, :], 0.0).then_inc(cst, 1)
        pool.wait_ge(cst, 2)
        nc.gpsimd.affine_select(out=ident[:, :], in_=ident[:, :], compare_op=ALU.not_equal, fill=1.0, base=0,
                                pattern=[[-1, P]], channel_multiplier=1).then_inc(cst, 1)
        nc.gpsimd.memset(eps[:, 0:1], 1e-6).then_inc(cst, 1)
        nc.gpsimd.memset(eps[:, 1:2], 1e-5).then_inc(cst, 1)
        sum_tiles(nc, pool, 0, S, xc, sq)
        layernorm_pool(nc, pool, 0, S, sq, xc, xn)

    @block.scalar
    def _(act):
        act.sem_inc(free[RING], 1)
        act.wait_ge(cst, 5)
        act.wait_ge(loads, 16 * 6)
        for c in range(NG):
            act.wait_ge(hidp, c + 1)
            if c >= 2:
                act.wait_ge(tabp, c - 1)
            for a in range(2):
                nc.scalar.activation(hid[:, c % 2, a, :], ring[c % 2][0:MH, a * HALF:a * HALF + CH], ACT.Gelu,
                                     bias=b1c[:, a:a + 1]).then_inc(hidr, 1)
            if c in LN_ACT:
                layernorm_act(nc, act, LN_ACT[c], filled, read, 0, r, S, xc, sq, std, eps[:, 0:1], xn)
            if c == W_AT:
                act.wait_ge(wload, 16)
            if 0 <= c - W_AT < KC:
                k = c - W_AT
                nc.scalar.activation(T["wh"][:, k, :], wtmp[:, k, :], ACT.Copy, scale=WS).then_inc(wh_ready, 1)

    @block.tensor
    def _(pe):
        def first_layer(c):
            if c >= 2:
                pe.wait_ge(hidr, 2 * (c - 1))
            for a in range(2):
                last = nc.tensor.matmul(ring[c % 2][0:MH, a * HALF:a * HALF + CH], w1s[:, a * MH:(a + 1) * MH],
                                        grid[:, c * CH:(c + 1) * CH], start=True, stop=True)
            last.then_inc(hidp, 1)

        pe.wait_ge(cst, 5)
        pe.wait_ge(loads, 16 * 6)
        pe.wait_ge(gridf, 1)
        first_layer(0)
        for c in range(NG):
            if c + 1 < NG:
                first_layer(c + 1)
            pe.wait_ge(hidr, 2 * (c + 1))
            if c >= 2:
                pe.wait_ge(tabf, 2 * (c - 1))
            at = (c % 2) * HALF
            for a in range(2):
                last = nc.tensor.matmul(ring[2][0:HEADS, at:at + CH], w2c[:, a, :], hid[:, c % 2, a, :],
                                        start=a == 0, stop=a == 1)
            last.then_inc(tabp, 1)
            if c in LN_PE:
                layernorm_pe(nc, pe, LN_PE[c], taken, 0, r, S, sq, mean_w, ident, rstd)
        pe.wait_ge(wp_in, 16 * 4)
        pe.wait_ge(tabf, 2 * NG)
        for m in range(KC):
            for p in range(PAIRS):
                last = nc.tensor.matmul(ring[2][:, m:m + 1], T["wp"][:, p, m * P:(m + 1) * P], bv[:, p:p + 1],
                                        start=p == 0, stop=p == PAIRS - 1)
        last.then_inc(pbp, 1)

    @block.vector
    def _(dve):
        dve.wait_ge(gridi, 1)
        dve.wait_ge(grid_in, 16)
        nc.vector.tensor_scalar(grid[:, :], grid[:, :], 1.0 / (HT - 1), None, ALU.mult).then_inc(gridf, 1)
        dve.wait_ge(loads, 16 * 6)
        nc.vector.tensor_scalar(T["qkb"][:, :], T["qkb"][:, :], WS, None, ALU.mult).then_inc(wdone, 1)
        for c in range(NG):
            dve.wait_ge(tabp, c + 1)
            half = ring[2][0:HEADS, (c % 2) * HALF:(c % 2) * HALF + CH]
            nc.vector.tensor_scalar(tab_s[:, c * CH:(c + 1) * CH], half, b2c[:, 0:1], None, ALU.add).then_inc(tabf, 1)
            whole = tabr_s[:, :]
            turned = bass.AP(whole.tensor, whole.offset + PTS - 1 - c * CH, [list(whole.ap[0]), [-1, CH]])
            nc.vector.tensor_scalar(turned, half, b2c[:, 0:1], 1.0 / SCALE, ALU.add, ALU.mult).then_inc(tabf, 1)
            if c in LN_DVE:
                layernorm_dve(nc, dve, LN_DVE[c], filled, read, 0, r, S, xc, std, rstd, xc)
            if 0 <= c - W_AT < KC:
                k = c - W_AT
                dve.wait_ge(wh_ready, k + 1)
                nc.vector.scalar_tensor_tensor(out=T["wl"][:, k, :], in0=wtmp[:, k, :], scalar=WS,
                                               in1=T["wh"][:, k, :], op0=ALU.mult, op1=ALU.subtract)\
                    .then_inc(wdone, 1)
        dve.wait_ge(pbp, 1)
        nc.vector.tensor_tensor(T["pb"][:, :], ring[2][:, 0:KC], pb0[:, :], ALU.add).then_inc(wdone, 1)


def attention(nc, ctx, sbuf, T, L, ident, mean_w, ring, acc, x_v, out_v, tab, tabr, win, winr, qk_d):
    def sem(name):
        return ctx.enter_context(nc.semaphore(name))

    first = Round(PROLOGUE, [0] * RING)
    body = Round(image_tiles(True), first.after, B - 1)
    final = Round(image_tiles(False), body.after)
    bias, wh, wl, wp, qkb, pb = (T[k] for k in ("bias", "wh", "wl", "wp", "qkb", "pb"))
    xc, xn, sq, std, rstd, eps = (L[k] for k in ("xc", "xn", "sq", "std", "rstd", "eps"))
    st = sbuf(ctx, "st", [P, 2, 2, N], F16)
    res2 = sbuf(ctx, "res2", [P, N])
    res = [st[:, i, :, :].rearrange("p s n -> p (s n)").bitcast(F32) for i in range(2)] + [res2[:, :]]
    q2 = sbuf(ctx, "q2", [P, 2, 2, N], F16)
    kh = sbuf(ctx, "kh", [P, 2, 2, N], F16)
    kl = sbuf(ctx, "kl", [P, 2, 2, N], F16)
    ur = sbuf(ctx, "ur", [P, 2, NR * WD], BF16)
    v = sbuf(ctx, "v", [P, NT, HEADS, 64])
    zp = sbuf(ctx, "zp", [P, Z, N])
    xo = sbuf(ctx, "xo", [P, PAIRS, N])
    cm = sbuf(ctx, "cm", [P, 2, 2 * NT])
    ct = sbuf(ctx, "ct", [2 * NT, 2, P], F16)
    rc = sbuf(ctx, "rc", [P, NT, 2])

    ready = [sem(f"ready{i}") for i in range(RING)]
    free = [sem(f"free{i}") for i in range(RING)]
    taken, filled, read = tile_waits(ring, ready, free)
    names = ("consts", "x_in", "xc_ready", "sq_ready", "summed", "rstd_ready", "xn_ready", "xh_ready", "xl_ready", "win_out",
             "winr_out", "sh_ready", "res_in", "ur_in", "p_ready", "pv_done", "osb_ready", "stored",
             "step", "image")
    S = {n: sem(n) for n in names}
    st_out = [sem(f"st_out{i}") for i in range(2)]
    qk_in = [sem(f"qk_in{i}") for i in range(2)]
    bias_in = [sem(f"bias_in{p}") for p in range(PAIRS)]
    max_in = [sem(f"max_in{i}") for i in range(2)]
    block = ctx.enter_context(nc.Block())
    QK_IN, NTILE = 16 * 6, PAIRS * NT * 2

    def tab_rows(t):
        return bass.AP(t.tensor, t.offset + WD - 1, [[ND * NDP, HEADS], [NDP, ND], [-1, WD], [1, WD]])

    def make_windows(sp, t, dst, out):
        sp.dma_start(dst.rearrange("c h a w -> h a c w"), tab_rows(t)).then_inc(S[out], 16)

    def load_bias(sp, p):
        for y in range(RT):
            at = (RT - 1 - y) * WD
            sp.dma_start(bias[y * WD:(y + 1) * WD, 2 * p:2 * p + 2, :],
                         win.rearrange("c h a w -> c h (a w)")[:, 2 * p:2 * p + 2, at:at + NR * WD])\
                .then_inc(bias_in[p], 16)

    def store_block(sp, t, im, r):
        read(sp, ("qk", t), r)
        i = QK_ORDER.index(t) % 2
        for s in range(2):
            sp.dma_start(qk_d[bass.ds(im, 1), s, t * P:(t + 1) * P, :].squeeze(0),
                         st[:, i, s, :]).then_inc(st_out[i], 16)

    def load_pair(sp, p, im):
        i, h = p % 2, 2 * p * D
        for s in range(2):
            rows = slice(s * D, (s + 1) * D)
            q = qk_d[bass.ds(im, 1), s, h:h + 2 * D, :].squeeze(0).rearrange("(h d) n -> d h n", d=D)
            sp.dma_start(q2[rows, i, :, :], q).then_inc(qk_in[i], 16)
            for part, dst in ((0, kh), (1, kl)):
                k = qk_d[bass.ds(im, 1), part, C + h:C + h + 2 * D, :].squeeze(0).rearrange("(h d) n -> d h n", d=D)
                sp.dma_start(dst[rows, i, :, :], k).then_inc(qk_in[i], 16)

    def load_window(sp, p):
        for y in range(RT):
            at = (RT - 1 - y) * WD
            sp.dma_start(ur[y * WD:(y + 1) * WD, :, :],
                         winr.rearrange("c h a w -> c h (a w)")[:, 2 * p:2 * p + 2, at:at + NR * WD])\
                .then_inc(S["ur_in"], 16)

    def max_rows(sp, p, r):
        read(sp, ("ct", p), r)
        for hh in range(2):
            sp.dma_start(q2[2 * D:2 * D + 1, p % 2, hh, :],
                         ct[hh * NT:(hh + 1) * NT, p % 2, :]).then_inc(max_in[p % 2], 16)

    @block.sync
    def _(sp):
        def image(b, r, prepare):
            sp.dma_start(xc[:, :, :], x_v[bass.ds(b + 1, 1)].squeeze(0) if prepare else out_v[0])\
                .then_inc(S["x_in"], 16)
            for kind, *at in image_steps(prepare):
                if kind == "qk":
                    store_block(sp, *at, b + 1, r)
                elif kind == "ct":
                    max_rows(sp, *at, r)
                    if at[0] + 1 < PAIRS or prepare:
                        load_window(sp, (at[0] + 1) % PAIRS)
                elif kind == "proj":
                    m, = at
                    read(sp, ("proj", m), r)
                    sp.dma_start(out_v[bass.ds(b, 1), :, m, :].squeeze(0), res[m]).then_inc(S["stored"], 16)
                elif kind == "s" and at[1:] == [1, NT - 1]:
                    p = at[0]
                    if p + 2 < PAIRS or prepare:
                        filled(sp, ("s", p, 1, NT - 1), r)
                        sp.sem_inc(S["image"], 1)
                        if p + 2 >= PAIRS:
                            for i in range(2):
                                sp.wait_ge(st_out[i], b * (32 * KC) + 32 * KC + (32 if p + 2 == PAIRS else 32 * KC))
                        load_pair(sp, (p + 2) % PAIRS, b + (p + 2) // PAIRS)
                    if p == PAIRS - 1:
                        sp.wait_ge(S["stored"], b * (16 * KC) + 1)
                        sp.sem_inc(S["image"], 1)
                        for m in range(KC):
                            sp.dma_start(res[m], x_v[bass.ds(b, 1), :, m, :].squeeze(0)).then_inc(S["res_in"], 16)

        sp.sem_inc(S["stored"], 1)
        make_windows(sp, tabr, winr, "winr_out")
        for n, (_, t) in enumerate(QK_TILES):
            store_block(sp, t, 0, first.at(0))
            if n == 1:
                for i in range(2):
                    sp.wait_ge(st_out[i], 32)
                load_pair(sp, 0, 0)
                sp.wait_ge(S["winr_out"], 16)
                load_window(sp, 0)
            if n == 3:
                make_windows(sp, tab, win, "win_out")
        for i in range(2):
            sp.wait_ge(st_out[i], 32 * KC)
        load_pair(sp, 1, 0)
        sp.wait_ge(S["win_out"], 16)
        load_bias(sp, 0)
        max_rows(sp, PAIRS, first.at(0))
        load_window(sp, 1)
        read(sp, V_TILES[-1], first.at(0))
        with sp.Fori(0, B - 1) as b:
            image(b, body.at(b), True)
        image(B - 1, final.at(0), False)
        sp.wait_ge(S["stored"], 16 * KC * B + 1)

    @block.gpsimd
    def _(pool):
        nc.gpsimd.memset(v[:, :, :, :], 1.0).then_inc(S["consts"], 1)
        pool.wait_ge(S["consts"], 1)
        nc.gpsimd.memset(kh[2 * D:P, :, :, :], CS).then_inc(S["consts"], 1)
        sum_tiles(nc, pool, 0, S, xc, sq)
        pool.wait_ge(S["win_out"], 16)
        for p in range(1, PAIRS):
            load_bias(pool, p)
        layernorm_pool(nc, pool, 0, S, sq, xc, xn)
        with pool.Fori(1, B) as b:
            sum_tiles(nc, pool, b, S, xc, sq)
            layernorm_pool(nc, pool, b, S, sq, xc, xn)

    @block.tensor
    def _(pe):
        def scores(p, hh, j, r):
            buf, done = taken(pe, ("s", p, hh, j), r)
            i = p % 2
            for f in range(2):
                cols = slice(f * HALF, (f + 1) * HALF)
                nc.tensor.matmul(buf[:, cols], kh[0:2 * D + 1, i, hh, j * P:(j + 1) * P],
                                 q2[0:2 * D + 1, i, hh, cols], start=True, stop=False)
                last = nc.tensor.matmul(buf[:, cols], kl[0:2 * D, i, hh, j * P:(j + 1) * P],
                                        q2[0:2 * D, i, hh, cols], start=False, stop=True)
            last.then_inc(done, 1)

        def max_scores(p, hh, i, r):
            buf, done = taken(pe, ("m", p, hh, i), r)
            for f in range(2):
                cols = slice(f * HALF, (f + 1) * HALF)
                last = nc.tensor.matmul(buf[:, cols], q2[0:2 * D, p % 2, hh, i * P:(i + 1) * P],
                                        kh[0:2 * D, p % 2, hh, cols], start=True, stop=True)
            last.then_inc(done, 1)

        def max_transpose(p, r):
            buf, done = taken(pe, ("ct", p), r)
            read(pe, ("m", p, 1, NT - 1), r, ("ct", p))
            nc.tensor.transpose(buf[0:2 * NT, 0:P], cm[:, p % 2, :], ident[:, :]).then_inc(done, 1)

        def values(p, j, f, b):
            k = 2 * NT * p + 2 * j
            if f == 0:
                pe.wait_ge(S["p_ready"], b * NTILE + k + 2)
                if j == 0 and p >= 1:
                    pe.wait_ge(S["osb_ready"], b * PAIRS + p)
            cols = slice(f * HALF, (f + 1) * HALF)
            for hh in range(2):
                last = nc.tensor.matmul(acc[64 * hh:64 * hh + 64, cols], v[:, j, 2 * p + hh, :],
                                        zp[:, (k + hh) % Z, cols], start=j == 0, stop=j == NT - 1)
            if f == 1:
                last.then_inc(S["pv_done"], 2)

        def sums_transpose(p, b, r):
            buf, done = taken(pe, ("ot", p), r)
            pe.wait_ge(S["osb_ready"], b * PAIRS + p + 1)
            for i in range(NT):
                last = nc.tensor.transpose(buf[:, i * P:(i + 1) * P], xo[:, p, i * P:(i + 1) * P], ident[:, :])
            last.then_inc(done, 1)

        def sums_broadcast(p, r):
            buf, done = taken(pe, ("rb", p), r)
            read(pe, ("ot", p), r, ("rb", p))
            for i in range(NT):
                for hh in range(2):
                    last = nc.tensor.matmul(buf[64 * hh:64 * hh + 64, i * P:(i + 1) * P],
                                            rc[:, i, hh:hh + 1].to_broadcast([P, 64]), ident[:, :],
                                            start=True, stop=True)
            last.then_inc(done, 1)

        terms = [(w, s, k) for w, s in ((wh, 0), (wh, 1), (wl, 0)) for k in range(KC)]

        def project_qk(t, r, b=None):
            buf, done = taken(pe, ("qk", t), r)
            if b is not None and t == QK_ORDER[0]:
                pe.wait_ge(S["xl_ready"], b * KC + KC)
            for f in range(2):
                cols = slice(f * HALF, (f + 1) * HALF)
                for n, (w, s, k) in enumerate(terms):
                    last = nc.tensor.matmul(buf[:, cols], w[:, k, t * P:(t + 1) * P], xn[:, s, k, cols],
                                            start=n == 0, stop=n == len(terms) - 1)
            last.then_inc(done, 1)

        def project_v(t, r):
            buf, done = taken(pe, ("v", t), r)
            for f in range(2):
                rows = slice((2 * t + f) * P, (2 * t + f + 1) * P)
                for n, (w, s, k) in enumerate(terms):
                    last = nc.tensor.matmul(buf[:, f * HALF:f * HALF + C], xn[:, s, k, rows], w[:, k, 2 * C:3 * C],
                                            start=n == 0, stop=n == len(terms) - 1)
            last.then_inc(done, 1)

        def project_out(m, r):
            buf, done = taken(pe, ("proj", m), r)
            if m == 0:
                read(pe, ("rb", PAIRS - 1), r, ("proj", 0))
            for f in range(2):
                cols = slice(f * HALF, (f + 1) * HALF)
                for p in range(PAIRS):
                    last = nc.tensor.matmul(buf[:, cols], wp[:, p, m * P:(m + 1) * P], xo[:, p, cols],
                                            start=p == 0, stop=p == PAIRS - 1)
            last.then_inc(done, 1)

        def image(b, r, prepare):
            for kind, *at in image_steps(prepare):
                if kind == "s":
                    p, hh, j = at
                    if (hh, j) == (0, 0):
                        pe.wait_ge(max_in[p % 2], b * 64 + 32 * (p // 2 + 1))
                    scores(p, hh, j, r)
                elif kind == "m":
                    p, hh, i = at
                    if (hh, i) == (0, 0):
                        pe.wait_ge(qk_in[p % 2], b * (2 * QK_IN) + QK_IN * (p // 2 + 1))
                    max_scores(p, hh, i, r)
                elif kind == "ct":
                    max_transpose(*at, r)
                elif kind == "pv":
                    values(*at, b)
                elif kind == "ot":
                    sums_transpose(*at, b, r)
                elif kind == "rb":
                    sums_broadcast(*at, r)
                elif kind == "qk":
                    project_qk(*at, r, b)
                elif kind == "v":
                    project_v(*at, r)
                elif kind == "proj":
                    project_out(*at, r)
                elif (kind,) in LN_TILES:
                    layernorm_pe(nc, pe, kind, taken, b, r, S, sq, mean_w, ident, rstd)

        r = first.at(0)
        for kind, *at in PROLOGUE:
            if kind == "qk":
                project_qk(*at, r)
            elif kind == "v":
                project_v(*at, r)
            elif kind == "m":
                if at[1:] == [0, 0]:
                    pe.wait_ge(S["consts"], 2)
                    pe.wait_ge(qk_in[0], QK_IN)
                max_scores(*at, r)
            else:
                max_transpose(*at, r)
        read(pe, ("v", NT // 2 - 1), r)
        with pe.Fori(0, B - 1) as b:
            image(b, body.at(b), True)
        image(B - 1, final.at(0), False)

    @block.scalar
    def _(act):
        def exps(p, hh, j, r):
            k = 2 * NT * p + 2 * j + hh
            read(act, ("s", p, hh, j), r)
            nc.scalar.activation(zp[:, k % Z, :], zp[:, k % Z, :], ACT.Exp).then_inc(S["p_ready"], 1)

        def max_evac(p, r):
            buf, done = filled(act, ("ct", p), r)
            nc.scalar.activation(ct[:, p % 2, :], buf[0:2 * NT, 0:P], ACT.Copy, scale=-1.0 / CS).then_inc(done, 1)

        def qk_high(t, im, r):
            buf, _ = filled(act, ("qk", t), r)
            n = QK_ORDER.index(t)
            if n >= 2:
                act.wait_ge(st_out[n % 2], im * (32 * KC) + 32 * (n // 2))
            nc.scalar.activation(st[:, n % 2, 0, :], buf[:, :], ACT.Identity, bias=qkb[:, t:t + 1])\
                .then_inc(S["sh_ready"], 1)

        def v_evac(t, r):
            buf, done = filled(act, ("v", t), r)
            for f in range(2):
                last = nc.scalar.activation(v[:, 2 * t + f, :, 0:D],
                                            buf[:, f * HALF:f * HALF + C].rearrange("p (h d) -> p h d", d=D),
                                            ACT.Copy, scale=1.0 / WS)
            last.then_inc(done, 1)

        def image(b, r, prepare):
            for kind, *at in image_steps(prepare):
                if kind == "s":
                    exps(*at, r)
                elif kind == "sums":
                    p, = at
                    act.wait_ge(S["pv_done"], b * NTILE + 2 * NT * (p + 1))
                    nc.scalar.activation(xo[:, p, :], acc[:, :], ACT.Copy).then_inc(S["osb_ready"], 1)
                elif kind == "ct":
                    max_evac(*at, r)
                elif kind == "qk":
                    if at[0] == QK_ORDER[0]:
                        act.wait_ge(S["stored"], b * (16 * KC) + 1)
                    qk_high(*at, b + 1, r)
                elif kind == "v":
                    v_evac(*at, r)
                elif (kind,) in LN_TILES:
                    layernorm_act(nc, act, kind, filled, read, b, r, S, xc, sq, std,
                                  eps[:, 0:1] if prepare else eps[:, 1:2], xn)

        for f in free:
            act.sem_inc(f, 1)
        r = first.at(0)
        for kind, *at in PROLOGUE:
            if kind == "qk":
                qk_high(*at, 0, r)
            elif kind == "v":
                act.wait_ge(S["consts"], 2)
                v_evac(*at, r)
            elif kind == "ct":
                max_evac(*at, r)
        with act.Fori(0, B - 1) as b:
            image(b, body.at(b), True)
        image(B - 1, final.at(0), False)

    @block.vector
    def _(dve):
        def softmax_in(p, hh, j, b, r):
            buf, done = filled(dve, ("s", p, hh, j), r)
            k = 2 * NT * p + 2 * j + hh
            if k >= Z:
                dve.wait_ge(S["pv_done"], b * NTILE + k - Z + 1)
            at = (NT - 1 - j) * RT * WD
            nc.vector.scalar_tensor_tensor(out=zp[:, k % Z, :], in0=buf[:, :], scalar=SCALE,
                                           in1=bias[:, 2 * p + hh, at:at + N], op0=ALU.mult, op1=ALU.add)\
                .then_inc(done, 1)

        def row_max(p, hh, i, r):
            buf, done = filled(dve, ("m", p, hh, i), r)
            at = (NT - 1 - i) * RT * WD
            n = hh * NT + i
            dve.sem_inc(S["step"], 1)
            nc.vector.tensor_tensor_reduce(out=buf[:, :], in0=buf[:, :], in1=ur[:, hh, at:at + N],
                                           scale=1.0, scalar=-3.0e38, op0=ALU.add, op1=ALU.max,
                                           accum_out=cm[:, p % 2, n:n + 1]).then_inc(done, 1)

        def qk_low(t, im, r):
            n = QK_ORDER.index(t)
            dve.wait_ge(S["sh_ready"], im * (2 * KC) + n + 1)
            buf, done = filled(dve, ("qk", t), r)
            nc.vector.scalar_tensor_tensor(out=st[:, n % 2, 1, :], in0=buf[:, :], scalar=qkb[:, t:t + 1],
                                           in1=st[:, n % 2, 0, :], op0=ALU.add, op1=ALU.subtract).then_inc(done, 1)

        def sums_inverse(p, r):
            buf, done = filled(dve, ("ot", p), r)
            nc.vector.reciprocal(rc[:, :, :], buf[:, :].rearrange("p (i c) -> p i c", c=P)[:, :, D:D + 65:64])\
                .then_inc(done, 1)

        def normalise(p, r):
            buf, done = filled(dve, ("rb", p), r)
            nc.vector.tensor_tensor(xo[:, p, :], xo[:, p, :], buf[:, :], ALU.mult).then_inc(done, 1)

        def image(b, r, prepare):
            late = []
            for kind, *at in image_steps(prepare):
                if kind == "s":
                    if at[1:] == [0, 0]:
                        dve.wait_ge(bias_in[at[0]], 16 * RT)
                    softmax_in(*at, b, r)
                    for t in late:
                        qk_low(t, b + 1, r)
                    late = []
                elif kind == "m":
                    p, hh, i = at
                    if (hh, i) == (0, 0):
                        dve.wait_ge(S["ur_in"], b * (64 * PAIRS) + 64 * (p + 1))
                    row_max(p, hh, i, r)
                elif kind == "ot":
                    sums_inverse(*at, r)
                elif kind == "rb":
                    normalise(*at, r)
                elif kind == "qk":
                    late += at
                elif kind == "proj":
                    m, = at
                    if m == 0:
                        dve.wait_ge(S["res_in"], b * (16 * KC) + 16 * KC)
                    buf, done = filled(dve, ("proj", m), r)
                    nc.vector.scalar_tensor_tensor(out=res[m], in0=buf[:, :], scalar=pb[:, m:m + 1],
                                                   in1=res[m], op0=ALU.add, op1=ALU.add).then_inc(done, 1)
                elif (kind,) in LN_TILES:
                    layernorm_dve(nc, dve, kind, filled, read, b, r, S, xc, std, rstd, xc)

        r = first.at(0)
        for kind, *at in PROLOGUE:
            if kind == "qk":
                qk_low(*at, 0, r)
            elif kind == "m":
                if at[1:] == [0, 0]:
                    dve.wait_ge(S["ur_in"], 64)
                row_max(*at, r)
        with dve.Fori(0, B - 1) as b:
            image(b, body.at(b), True)
        image(B - 1, final.at(0), False)


def layernorm_pe(nc, pe, kind, taken, im, r, S, sq, mean_w, ident, rstd):
    buf, done = taken(pe, (kind,), r)
    if kind == "mean":
        pe.wait_ge(S["summed"], im * (2 * KC - 2) + KC - 1)
        for f in range(2):
            cols = slice(f * HALF, (f + 1) * HALF)
            last = nc.tensor.matmul(buf[:, cols], mean_w[:, :], sq[:, 0, cols], start=True, stop=True)
    elif kind == "var":
        pe.wait_ge(S["summed"], im * (2 * KC - 2) + 2 * KC - 2)
        for i in range(NT):
            last = nc.tensor.matmul(buf[:, i:i + 1], sq[:, 0, i * P:(i + 1) * P], mean_w[:, 0:1],
                                    start=True, stop=True)
    else:
        pe.wait_ge(S["rstd_ready"], im + 1)
        for i in range(NT):
            last = nc.tensor.matmul(buf[:, i * P:(i + 1) * P], rstd[:, i:i + 1].to_broadcast([P, P]), ident[:, :],
                                    start=True, stop=True)
    last.then_inc(done, 1)


def layernorm_act(nc, act, kind, filled, read, im, r, S, xc, sq, std, eps, xn):
    if kind == "var":
        buf, done = filled(act, ("var",), r)
        nc.scalar.activation(std[:, :], buf[:, 0:NT], ACT.Sqrt, bias=eps).then_inc(done, 1)
        return
    for k in range(KC):
        if k == KC - 1:
            read(act, (kind,), r)
        if kind == "mean":
            if k < KC - 1:
                act.wait_ge(S["xc_ready"], im * (KC - 1) + k + 1)
            nc.scalar.activation(sq[:, k, :], xc[:, k, :], ACT.Square).then_inc(S["sq_ready"], 1)
        else:
            if k < KC - 1:
                act.wait_ge(S["xn_ready"], im * (KC - 1) + k + 1)
            nc.scalar.activation(xn[:, 0, k, :], xc[:, k, :], ACT.Copy).then_inc(S["xh_ready"], 1)


def layernorm_dve(nc, dve, kind, filled, read, im, r, S, x, std, rstd, xc, ks=range(KC)):
    if kind == "var":
        read(dve, ("var",), r)
        nc.vector.reciprocal(rstd[:, :], std[:, :]).then_inc(S["rstd_ready"], 1)
        return
    for k in ks:
        buf, done = filled(dve, (kind,), r)
        if kind == "mean":
            nc.vector.tensor_tensor(xc[:, k, :], x[:, k, :], buf[:, :], ALU.subtract)\
                .then_inc(S["xc_ready"] if k < KC - 1 else done, 1)
        else:
            if k == 0:
                dve.wait_ge(S["sq_ready"], im * KC + KC)
            nc.vector.tensor_tensor(xc[:, k, :], xc[:, k, :], buf[:, :], ALU.mult)\
                .then_inc(S["xn_ready"] if k < KC - 1 else done, 1)


def sum_tiles(nc, pool, im, S, x, sq):
    pool.wait_ge(S["x_in"], im * 16 + 16)
    for k in range(1, KC):
        if k > 1:
            pool.wait_ge(S["summed"], im * (2 * KC - 2) + k - 1)
        nc.gpsimd.tensor_tensor(sq[:, 0, :], x[:, 0, :] if k == 1 else sq[:, 0, :], x[:, k, :], ALU.add)\
            .then_inc(S["summed"], 1)


def layernorm_pool(nc, pool, im, S, sq, xc, xn):
    for k in range(1, KC):
        pool.wait_ge(S["sq_ready"], im * KC + k + 1)
        if k > 1:
            pool.wait_ge(S["summed"], im * (2 * KC - 2) + KC - 1 + k - 1)
        nc.gpsimd.tensor_tensor(sq[:, 0, :], sq[:, 0, :], sq[:, k, :], ALU.add).then_inc(S["summed"], 1)
    for k in range(KC):
        pool.wait_ge(S["xh_ready"], im * KC + k + 1)
        nc.gpsimd.tensor_tensor(xn[:, 1, k, :], xc[:, k, :], xn[:, 0, k, :], ALU.subtract).then_inc(S["xl_ready"], 1)


def binary_weights(nc, ctx, sbuf, sem, T, rooms, ident, mean_w, ring, acc, W1, b1, W2, b2):
    LOT = 6
    mats = ((W1, FK, C, G1, T["w1t"]), (W2, KC, FF, G2, T["w2t"]))
    w = [room[:, 0:m[1] * m[2]].rearrange("p (k n) -> p k n", n=m[2]) for room, m in zip(rooms, mats)]
    sg = [sbuf(ctx, f"sg{i}", [P, m[1], m[2]], F16) for i, m in enumerate(mats)]
    mask = [sbuf(ctx, f"mask{i}", [P, m[1], GROUPS]) for i, m in enumerate(mats)]
    prod = [sbuf(ctx, f"prod{i}", [P, m[1], GROUPS]) for i, m in enumerate(mats)]
    rs = [sbuf(ctx, f"rs{i}", [P, m[1]]) for i, m in enumerate(mats)]
    gs = [sbuf(ctx, f"gs{i}", [P, GROUPS]) for i, m in enumerate(mats)]
    gm = [sbuf(ctx, f"gm{i}", [P, GROUPS]) for i, m in enumerate(mats)]
    rm = [sbuf(ctx, f"rm{i}", [P, m[1]]) for i, m in enumerate(mats)]
    live = [sbuf(ctx, f"live{i}", [P, m[1]]) for i, m in enumerate(mats)]
    idh = sbuf(ctx, "idh", [P, P], F16)
    w_in = [sem(f"w{i}_in") for i in range(2)]
    masks, sums, group, chain, signs, zeroed, tp, tc = (
        sem(n) for n in ("masks", "sums", "group", "chain", "signs", "zeroed", "tp", "tc"))
    lots = [[(0, r + n, c) for n in range(LOT)] for r in range(0, FK, LOT) for c in range(KC)]
    lots += [[(1, r, c + n) for n in range(LOT // KC) for r in range(KC)] for c in range(0, FK, LOT // KC)]

    def load(sp):
        for i, m in enumerate(mats):
            sp.dma_start(w[i], m[0].rearrange("(k p) n -> p k n", p=P)).then_inc(w_in[i], 16)
        with nc.allow_non_contiguous_dma(reason="biases by partition"):
            sp.dma_start(T["b1s"][:, :], b1.rearrange("(k p) -> p k", p=P)).then_inc(T["b_in"], 16)
            sp.dma_start(T["b2s"][:, :], b2.rearrange("(k p) -> p k", p=P)).then_inc(T["b_in"], 16)

    def group_masks(pool):
        n = 0
        for i, m in enumerate(mats):
            nc.gpsimd.memset(mask[i][:, :, :], 1.0).then_inc(masks, 1)
            for base, mult in ((0, 1), (m[3] - 1, -1)):
                n += 1
                pool.wait_ge(masks, n)
                nc.gpsimd.affine_select(out=mask[i][:, :, :], in_=mask[i][:, :, :], compare_op=ALU.is_ge, fill=0.0,
                                        base=base, pattern=[[mult * P, m[1]], [-mult * m[3], GROUPS]],
                                        channel_multiplier=mult).then_inc(masks, 1)
            n += 1

    def take_signs(act):
        nc.scalar.activation(idh[:, :], ident[:, :], ACT.Copy).then_inc(signs, 1)
        for i, m in enumerate(mats):
            act.wait_ge(chain, 6 * (i + 1))
            for r in range(m[1]):
                nc.scalar.activation(sg[i][:, r, :], w[i][:, r, :], ACT.Sign, bias=rm[i][:, r:r + 1]).then_inc(signs, 1)

    def row_means(dve):
        dve.wait_ge(masks, 6)
        n = 0

        def link(ins):
            nonlocal n
            n += 1
            ins.then_inc(chain, 1)
            dve.wait_ge(chain, n)

        for i, m in enumerate(mats):
            dve.wait_ge(w_in[i], 16)
            link(nc.vector.tensor_reduce(out=rs[i][:, :], in_=w[i], axis=AX_X, op=ALU.add))
            link(nc.vector.tensor_tensor(prod[i][:, :, :], mask[i][:, :, :],
                                         rs[i][:, :].unsqueeze(2).to_broadcast([P, m[1], GROUPS]), ALU.mult))
            nc.vector.tensor_reduce(out=gs[i][:, :], in_=prod[i][:, :, :].rearrange("p k g -> p g k"), axis=AX_X,
                                    op=ALU.add).then_inc(sums, 1)
            dve.wait_ge(group, i + 1)
            link(nc.vector.tensor_scalar(gm[i][:, :], group_sum(i), -float(C) / (m[3] * m[2]), None, ALU.mult))
            link(nc.vector.tensor_tensor(prod[i][:, :, :], mask[i][:, :, :],
                                         gm[i][:, :].unsqueeze(1).to_broadcast([P, m[1], GROUPS]), ALU.mult))
            link(nc.vector.tensor_reduce(out=live[i][:, :], in_=mask[i][:, :, :], axis=AX_X, op=ALU.add))
            link(nc.vector.tensor_reduce(out=rm[i][:, :], in_=prod[i][:, :, :], axis=AX_X, op=ALU.add))

    def group_sum(i):
        return ring[i][:, 0:GROUPS]

    def group_sums(pe):
        for i in range(2):
            pe.wait_ge(sums, i + 1)
            nc.tensor.matmul(group_sum(i), mean_w[:, :], gs[i][:, :], start=True, stop=True).then_inc(group, 1)

    def bank(q):
        at = (q % 2) * HALF
        return acc[:, at:at + HALF].bitcast(F16)

    def zero_rows(dve, i):
        r = mats[i][1] - 1
        dve.wait_ge(signs, 1 + FK + i * KC)
        nc.vector.tensor_scalar(sg[i][:, r, :], sg[i][:, r, :], live[i][:, r:r + 1], None, ALU.mult)\
            .then_inc(zeroed, 1)

    def turn_lot(pe, q):
        if q >= 2:
            pe.wait_ge(tc, q - 1)
        for n, (i, r, c) in enumerate(lots[q]):
            if n == 0:
                pe.wait_ge(signs, 1 + i * FK + max(t[1] for t in lots[q]) + 1)
                if r + LOT == FK or i == 1:
                    pe.wait_ge(zeroed, i + 1)
            last = nc.tensor.transpose(bank(q)[:, n * P:(n + 1) * P], sg[i][:, r, c * P:(c + 1) * P], idh[:, :])
        last.then_inc(tp, 1)

    def copy_lot(dve, q):
        i, r, c = lots[q][0]
        dve.wait_ge(tp, q + 1)
        dst = T["w1t"][:, c, r * P:(r + LOT) * P] if i == 0 else T["w2t"][:, c:c + LOT // KC, :]\
            .rearrange("p c n -> p (c n)")
        nc.vector.tensor_copy(dst, bank(q)[:, 0:LOT * P]).then_inc(tc, 1)

    def turned(pe, n):
        pe.wait_ge(tc, n)

    first = sum(lot[0][0] == 0 for lot in lots)
    return (first, len(lots), load, group_masks, take_signs, row_means, group_sums, zero_rows, turn_lot, copy_lot,
            turned)


def feed_forward(nc, ctx, sbuf, T, L, ident, mean_w, ring, acc, W1, b1, W2, b2, out_v):
    def sem(name):
        return ctx.enter_context(nc.semaphore(name))

    own = set(LN_TILES)
    first = Round(F1_TILES, [0] * (RING + 1), 1, own)
    body = Round(F2_TILES + LN_TILES + F1_TILES, first.after, FB - 1, own)
    final = Round(F2_TILES, body.after, 1, own)
    w1t, w2t, b1s, b2s = (T[k] for k in ("w1t", "w2t", "b1s", "b2s"))
    NH = 4
    LN_PE = {0: "mean", 6: "var", 8: "rstd"}
    LN_ACT = {5: "mean", 7: "var", 11: "rstd"}
    LN_DVE = {2: ("mean", [0]), 3: ("mean", [1]), 4: ("mean", [2]), 6: ("var", []),
              9: ("rstd", [0]), 10: ("rstd", [1]), 11: ("rstd", [2])}
    t = sbuf(ctx, "t", [P, 2, KC, N])
    xc, xn, std, rstd, eps = (L[k] for k in ("xc", "xn", "std", "rstd", "eps"))
    sq = sbuf(ctx, "fsq", [P, KC, N])
    y = sbuf(ctx, "y", [P, FK, N])
    y2 = sbuf(ctx, "y2", [P, KC, N])
    h = sbuf(ctx, "h", [P, NH, 2, N], F16)
    am = sbuf(ctx, "am", [P, 2, FK])
    am1 = sbuf(ctx, "am1", [P, 2])
    gam = sbuf(ctx, "gam", [P, 2])
    ge = sbuf(ctx, "ge", [P, 2])
    gr = sbuf(ctx, "gr", [P, 2])
    sc = sbuf(ctx, "sc", [P, 2])
    ready = [sem(f"fready{i}") for i in range(RING + 1)]
    free = [sem(f"ffree{i}") for i in range(RING + 1)]
    taken, filled, read = tile_waits([*ring, acc], ready, free)
    names = ("t_in", "x_in", "xc_ready", "sq_ready", "summed", "rstd_ready", "xn_ready", "xh_ready", "xl_ready",
             "am_ready0", "am_ready1", "gam_ready0", "gam_ready1", "chain0", "chain1", "s_ready0", "s_ready1",
             "max0", "max1", "g_ready", "hh_ready", "hl_ready", "h_used", "clipped", "t_ready", "stored", "step",
             "image")
    S = {n: sem("f_" + n) for n in names}
    T["b_in"] = sem("b_in")
    flat = y[:, :, :].rearrange("p k n -> p (k n)")
    (FIRST_LOTS, LOTS, load_weights, group_masks, take_signs, row_means, group_sums, zero_rows, turn_lot, copy_lot,
     turned) = binary_weights(nc, ctx, sbuf, sem, T, (flat[:, 0:FK * N // 2], flat[:, FK * N // 2:]), ident, mean_w,
                              ring, acc, W1, b1, W2, b2)
    block = ctx.enter_context(nc.Block())
    assert FB % 2 == 1 and FB > 2

    def in_pairs(eng, image, last):
        with eng.Fori(0, FB - 1, 2) as b:
            for i in range(2):
                image(b + i, i, body.at(b + i), True)
        last(image)

    def final_image(image):
        image(FB - 1, (FB - 1) % 2, final.at(0), False)

    @block.sync
    def _(sp):
        def image(b, i, r, more):
            if more:
                sp.dma_start(t[:, 1 - i, :, :], out_v[bass.ds(b + 1, 1)].squeeze(0)).then_inc(S["x_in"], 16)
            sp.wait_ge(S["t_ready"], b * KC + KC)
            sp.dma_start(out_v[bass.ds(b, 1)].squeeze(0), t[:, i, :, :]).then_inc(S["stored"], 16)
            sp.wait_ge(S["stored"], b * 16 + 16)
            sp.sem_inc(S["image"], 1)

        load_weights(sp)
        sp.dma_start(t[:, 0, :, :], out_v[0]).then_inc(S["t_in"], 16)
        in_pairs(sp, image, final_image)
        sp.wait_ge(S["stored"], 16 * FB)

    @block.gpsimd
    def _(pool):
        def all_max(b, s):
            pool.wait_ge(S[f"am_ready{s}"], b + 1)
            pool.sem_inc(S["step"], 1)
            nc.gpsimd.partition_all_reduce(gam[:, s:s + 1], am1[:, s:s + 1], P, ABSMAX)\
                .then_inc(S[f"gam_ready{s}"], 1)

        group_masks(pool)
        with pool.Fori(0, FB - 1, 2) as b:
            for i in range(2):
                sum_tiles(nc, pool, b + i, S, t[:, 1 - i, :, :], sq)
                all_max(b + i, 0)
                layernorm_pool(nc, pool, b + i, S, sq, xc, xn)
                all_max(b + i, 1)
        all_max(FB - 1, 0)
        all_max(FB - 1, 1)

    @block.tensor
    def _(pe):
        def first_layer(r, b=None):
            for o in range(FK):
                buf, done = taken(pe, ("f1", o), r)
                for s in range(2):
                    if b is not None and o == 0:
                        pe.wait_ge(S["xl_ready" if s else "xh_ready"], b * KC + KC)
                    for f in range(2):
                        cols = slice(f * HALF, (f + 1) * HALF)
                        for k in range(KC):
                            last = nc.tensor.matmul(buf[:, cols], w1t[:, k, o * P:(o + 1) * P], xn[:, s, k, cols],
                                                    start=s == 0 and k == 0, stop=s == 1 and k == KC - 1)
                last.then_inc(done, 1)
                if b is None and FIRST_LOTS + o < LOTS:
                    turn_lot(pe, FIRST_LOTS + o)

        def image(b, i, r, more):
            for k in range(FK):
                if more and k in LN_PE:
                    layernorm_pe(nc, pe, LN_PE[k], taken, b, r, S, sq, mean_w, ident, rstd)
                if k == 0:
                    accs = [taken(pe, ("f2", m), r) for m in range(KC)]
                pe.wait_ge(S["hl_ready"], b * FK + k + 1)
                for m in range(KC):
                    for f in range(2):
                        cols = slice(f * HALF, (f + 1) * HALF)
                        for s in range(2):
                            last = nc.tensor.matmul(accs[m][0][:, cols], w2t[:, k, m * P:(m + 1) * P],
                                                    h[:, k % NH, s, cols], start=k == 0 and s == 0,
                                                    stop=k == FK - 1 and s == 1)
                    if k == FK - 1:
                        last.then_inc(accs[m][1], 1)
                if k < FK - 1:
                    last.then_inc(S["h_used"], 1)
            if more:
                first_layer(r, b)

        group_sums(pe)
        for q in range(FIRST_LOTS):
            turn_lot(pe, q)
        turned(pe, FIRST_LOTS)
        first_layer(first.at(0))
        turned(pe, LOTS)
        in_pairs(pe, image, final_image)

    @block.scalar
    def _(act):
        def first_layer(r):
            for o in range(FK):
                buf, done = filled(act, ("f1", o), r)
                nc.scalar.activation(y[:, o, :], buf[:, :], ACT.Identity, bias=b1s[:, o:o + 1]).then_inc(done, 1)

        def image(b, i, r, more):
            act.wait_ge(S["s_ready0"], b + 1)
            for k in range(FK):
                nc.scalar.activation(y[:, k, :], y[:, k, :], ACT.Gelu, scale=sc[:, 0:1]).then_inc(S["g_ready"], 1)
                if more and k in LN_ACT:
                    layernorm_act(nc, act, LN_ACT[k], filled, read, b, r, S, xc, sq, std, eps[:, 1:2], xn)
            for m in range(KC):
                buf, done = filled(act, ("f2", m), r)
                nc.scalar.activation(y2[:, m, :], buf[:, :], ACT.Identity, bias=b2s[:, m:m + 1]).then_inc(done, 1)
            if more:
                first_layer(r)

        for f in free:
            act.sem_inc(f, 1)
        take_signs(act)
        act.wait_ge(T["b_in"], 32)
        first_layer(first.at(0))
        in_pairs(act, image, final_image)

    @block.vector
    def _(dve):
        def largest(src, s, o):
            nc.vector.tensor_reduce(out=am[:, s, o:o + 1], in_=src, axis=AX_X, op=ALU.max,
                                    apply_absolute_value=True).then_inc(S[f"max{s}"], 1)

        def scale_of(b, s, n):
            dve.wait_ge(S[f"max{s}"], b * n + n)
            nc.vector.tensor_reduce(out=am1[:, s:s + 1], in_=am[:, s, 0:n], axis=AX_X, op=ALU.max)\
                .then_inc(S[f"am_ready{s}"], 1)
            dve.wait_ge(S[f"gam_ready{s}"], b + 1)
            nc.vector.tensor_scalar(ge[:, s:s + 1], gam[:, s:s + 1], QEPS, None, ALU.add).then_inc(S[f"chain{s}"], 1)
            dve.wait_ge(S[f"chain{s}"], b * 2 + 1)
            nc.vector.reciprocal(gr[:, s:s + 1], ge[:, s:s + 1]).then_inc(S[f"chain{s}"], 1)
            dve.wait_ge(S[f"chain{s}"], b * 2 + 2)
            nc.vector.tensor_scalar(sc[:, s:s + 1], gr[:, s:s + 1], QB, None, ALU.mult).then_inc(S[f"s_ready{s}"], 1)

        def first_layer(r, lots=False):
            for o in range(FK):
                read(dve, ("f1", o), r)
                largest(y[:, o, :], 0, o)
                if lots and FIRST_LOTS + o < LOTS:
                    copy_lot(dve, FIRST_LOTS + o)

        def hidden(b, k):
            dve.wait_ge(S["g_ready"], b * FK + k + 1)
            if k >= NH:
                dve.wait_ge(S["h_used"], b * (FK - 1) + k - NH + 1)
            nc.vector.tensor_scalar(h[:, k % NH, 0, :], y[:, k, :], CLIP, None, ALU.min).then_inc(S["hh_ready"], 1)
            dve.wait_ge(S["hh_ready"], b * FK + k + 1)
            nc.vector.scalar_tensor_tensor(out=h[:, k % NH, 1, :], in0=y[:, k, :], scalar=CLIP,
                                           in1=h[:, k % NH, 0, :], op0=ALU.min, op1=ALU.subtract)\
                .then_inc(S["hl_ready"], 1)

        def image(b, i, r, more):
            for k in range(FK):
                hidden(b, k)
                if more and k in LN_DVE:
                    kind, ks = LN_DVE[k]
                    layernorm_dve(nc, dve, kind, filled, read, b, r, S, t[:, 1 - i, :, :], std, rstd, xc, ks)
            for m in range(KC):
                read(dve, ("f2", m), r)
                largest(y2[:, m, :], 1, m)
            scale_of(b, 1, KC)
            dve.wait_ge(S["s_ready1"], b + 1)
            for m in range(KC):
                nc.vector.tensor_scalar(y2[:, m, :], y2[:, m, :], sc[:, 1:2], CLIP, ALU.mult, ALU.min)\
                    .then_inc(S["clipped"], 1)
            for m in range(KC):
                dve.wait_ge(S["clipped"], b * KC + m + 1)
                nc.vector.scalar_tensor_tensor(out=t[:, i, m, :], in0=y2[:, m, :], scalar=-CLIP, in1=t[:, i, m, :],
                                               op0=ALU.max, op1=ALU.add).then_inc(S["t_ready"], 1)
            if more:
                first_layer(r)
                scale_of(b + 1, 0, FK)

        row_means(dve)
        zero_rows(dve, 0)
        for q in range(FIRST_LOTS):
            copy_lot(dve, q)
        zero_rows(dve, 1)
        first_layer(first.at(0), True)
        scale_of(0, 0, FK)
        dve.wait_ge(S["t_in"], 16)
        in_pairs(dve, image, final_image)


_INS = ["x", "L0_conv_qkv_w", "L0_conv_qkv_b", "L0_conv_proj_w", "L0_conv_proj_b", "L0_conv_mlp_w1",
        "L0_conv_mlp_b1", "L0_conv_mlp_w2", "L0_conv_mlp_b2", "L0_ffn_W1", "L0_ffn_b1", "L0_ffn_W2", "L0_ffn_b2"]
_OUTS = [((B, C, HT, WD), "float32")]


def kernel(**inputs):
    import numpy as _np
    import concourse.bacc as _bacc
    from concourse import mybir as _mybir
    from concourse.bass_utils import run_bass_kernel_spmd as _run

    nc = _bacc.Bacc("TRN2", target_bir_lowering=False, num_devices=1)
    arrays, args = {}, []
    for name in _INS:
        a = _np.ascontiguousarray(inputs[name])
        arrays[f"in_{name}_dram"] = a
        args.append(nc.dram_tensor(f"in_{name}_dram", a.shape, _mybir.dt.from_np(a.dtype), kind="ExternalInput").ap())
    for i, (shape, dtype) in enumerate(_OUTS):
        dt = _mybir.dt.from_np(_np.dtype(dtype))
        args.append(nc.dram_tensor(f"out_{i}_dram", shape, dt, kind="ExternalOutput").ap())
    metaformer(nc, *args)
    r = _run(nc, [arrays], core_ids=[0])
    got = tuple(r.results[0][f"out_{i}_dram"] for i in range(len(_OUTS)))
    return got[0]
```
